# Optimizing a Trainium2 kernel written in Bass

```python
import numpy as np
import jax
import jax.numpy as jnp

def _softmax(x, axis=-1):
    return jax.nn.softmax(x, axis=axis)
def _gelu(x):
    return jax.nn.gelu(x, approximate=True)
def _silu(x):
    return jax.nn.silu(x)
def _sigmoid(x):
    return jax.nn.sigmoid(x)
def _layernorm(x, axis=-1, eps=1e-5):
    m = jnp.mean(x, axis=axis, keepdims=True)
    v = jnp.var(x, axis=axis, keepdims=True)
    return (x - m) / jnp.sqrt(v + eps)
def _scatter_add(tgt, idx, src, axis=0):
    return tgt.at[idx].add(src)
def _segment_sum(src, seg, n):
    return jax.ops.segment_sum(src, seg, n)

kernel_name = 'mk_adj_ffn_d1_adj_256_03cdb2'

def setup_inputs(seed: int = 0):
    np.random.seed(seed)
    _w = jnp.asarray
    def _rec_inputs():
        import jax
        import jax.numpy as jnp
        _gk = jax.random.key(seed)
        x = -0.0005207 + 1.001 * jax.random.normal(jax.random.fold_in(_gk, 1), (4096, 256), jnp.float32)
        _a = jax.random.bernoulli(jax.random.fold_in(_gk, 2), 0.000976562, (4096, 4096))
        _a = jnp.logical_or(_a, jnp.swapaxes(_a, -1, -2))
        _a = jnp.logical_or(_a, jnp.eye(4096, dtype=bool))
        _af = _a.astype(jnp.float32)
        adj = _af
        return x, adj
    x, adj = _rec_inputs()
    def _L0_gnn_setup():
        import jax, jax.numpy as jnp
        import numpy as np
        NEG_INF = -9000000000000000.0
        ALPHA = 0.2
        key = jax.random.key(seed)
        ks = jax.random.split(key, 8)
        N, F = (8192, 256)
        h = jax.random.normal(ks[0], (N, F), dtype=jnp.float32)
        adj = jax.random.randint(ks[1], (N, N), 0, 2).astype(jnp.float32)
        W = jax.random.normal(ks[2], (F, F), dtype=jnp.float32) * 0.05
        a = jax.random.normal(ks[3], (2 * F, 1), dtype=jnp.float32) * 0.05
        w_ih = jax.random.normal(ks[4], (3 * F, F), dtype=jnp.float32) * 0.05
        w_hh = jax.random.normal(ks[5], (3 * F, F), dtype=jnp.float32) * 0.05
        b_ih = jax.random.normal(ks[6], (3 * F,), dtype=jnp.float32) * 0.05
        b_hh = jax.random.normal(ks[7], (3 * F,), dtype=jnp.float32) * 0.05
        return {'h': h, 'adj': adj, 'W': W, 'a': a, 'w_ih': w_ih, 'w_hh': w_hh, 'b_ih': b_ih, 'b_hh': b_hh}
    _L0_gnn_all = _L0_gnn_setup()
    _L0_gnn_in = {k: v for k, v in _L0_gnn_all.items() if k in ('W', 'a', 'w_ih', 'w_hh', 'b_ih', 'b_hh', )}
    del _L0_gnn_all

    def _L0_ffn_setup():
        import jax, jax.numpy as jnp
        import numpy as np
        D_MODEL = 256
        N_EXPERTS = 16
        HIDDEN = 512
        SCALE = 0.02
        key = jax.random.key(seed)
        ks = jax.random.split(key, 5)
        x = jax.random.normal(ks[0], (4, 8192, D_MODEL), dtype=jnp.float32)
        gate_w = jax.random.normal(ks[1], (D_MODEL, N_EXPERTS), dtype=jnp.float32) * SCALE
        gate_b = jnp.zeros((N_EXPERTS,), dtype=jnp.float32)
        w1 = jax.random.normal(ks[2], (N_EXPERTS, D_MODEL, HIDDEN), dtype=jnp.float32) * SCALE
        w2 = jax.random.normal(ks[3], (N_EXPERTS, D_MODEL, HIDDEN), dtype=jnp.float32) * SCALE
        w3 = jax.random.normal(ks[4], (N_EXPERTS, HIDDEN, D_MODEL), dtype=jnp.float32) * SCALE
        return {'x': x, 'gate_w': gate_w, 'gate_b': gate_b, 'w1': w1, 'w2': w2, 'w3': w3}
    _L0_ffn_all = _L0_ffn_setup()
    _L0_ffn_in = {k: v for k, v in _L0_ffn_all.items() if k in ('gate_w', 'gate_b', 'w1', 'w2', 'w3', )}
    del _L0_ffn_all

    return {
        "x": x,
        "adj": adj,
        "L0_gnn_W": _L0_gnn_in["W"],
        "L0_gnn_a": _L0_gnn_in["a"],
        "L0_gnn_w_ih": _L0_gnn_in["w_ih"],
        "L0_gnn_w_hh": _L0_gnn_in["w_hh"],
        "L0_gnn_b_ih": _L0_gnn_in["b_ih"],
        "L0_gnn_b_hh": _L0_gnn_in["b_hh"],
        "L0_ffn_gate_w": _L0_ffn_in["gate_w"],
        "L0_ffn_gate_b": _L0_ffn_in["gate_b"],
        "L0_ffn_w1": _L0_ffn_in["w1"],
        "L0_ffn_w2": _L0_ffn_in["w2"],
        "L0_ffn_w3": _L0_ffn_in["w3"],
    }

def reference(x, adj, L0_gnn_W, L0_gnn_a, L0_gnn_w_ih, L0_gnn_w_hh, L0_gnn_b_ih, L0_gnn_b_hh, L0_ffn_gate_w, L0_ffn_gate_b, L0_ffn_w1, L0_ffn_w2, L0_ffn_w3):
    import jax
    import jax.numpy as jnp
    def _L0_gnn_ref(h, adj, W, a, w_ih, w_hh, b_ih, b_hh):
        import jax, jax.numpy as jnp
        import numpy as np
        NEG_INF = -9000000000000000.0
        ALPHA = 0.2
        F_out = W.shape[1]
        Wh = h @ W
        src = Wh @ a[:F_out]
        dst = Wh @ a[F_out:]
        e = jax.nn.leaky_relu(src + dst.T, ALPHA)
        att = jnp.where(adj > 0, e, NEG_INF)
        att = jax.nn.softmax(att, axis=1)
        h_prime = att @ Wh
        gi = h_prime @ w_ih.T + b_ih
        gh = h @ w_hh.T + b_hh
        i_r, i_z, i_n = jnp.split(gi, 3, axis=1)
        h_r, h_z, h_n = jnp.split(gh, 3, axis=1)
        r = jax.nn.sigmoid(i_r + h_r)
        z = jax.nn.sigmoid(i_z + h_z)
        n = jnp.tanh(i_n + r * h_n)
        return (1.0 - z) * n + z * h

    def _L0_ffn_ref(x, gate_w, gate_b, w1, w2, w3):
        import jax, jax.numpy as jnp
        import numpy as np
        D_MODEL = 256
        N_EXPERTS = 16
        HIDDEN = 512
        SCALE = 0.02
        n_experts = w1.shape[0]
        logits = jnp.einsum('bsd,de->bse', x, gate_w) + gate_b
        probs = jax.nn.softmax(logits, axis=-1)
        top_probs, top_idx = jax.lax.top_k(probs, 2)
        top_probs = top_probs / jnp.sum(top_probs, axis=-1, keepdims=True)
        dispatch = jnp.sum(jax.nn.one_hot(top_idx, n_experts, dtype=x.dtype) * top_probs[..., None], axis=-2)
        h1 = jnp.einsum('bsd,edh->bseh', x, w1)
        h2 = jnp.einsum('bsd,edh->bseh', x, w2)
        hidden = jax.nn.silu(h1) * h2
        expert_out = jnp.einsum('bseh,eho->bseo', hidden, w3)
        return jnp.einsum('bseo,bse->bso', expert_out, dispatch)

    x = x + _L0_gnn_ref(_layernorm(x, axis=-1), adj, L0_gnn_W, L0_gnn_a, L0_gnn_w_ih, L0_gnn_w_hh, L0_gnn_b_ih, L0_gnn_b_hh)
    x = x + _L0_ffn_ref((_layernorm(x, axis=-1))[None], L0_ffn_gate_w, L0_ffn_gate_b, L0_ffn_w1, L0_ffn_w2, L0_ffn_w3)[0]
    return x


_drawn_inputs = setup_inputs


def setup_inputs(seed=0):
    import zlib

    import numpy as np

    out = dict(_drawn_inputs(seed))
    spreads = {'L0_ffn_gate_b': (0.0, 0.8)}
    factors = {'L0_gnn_b_ih': 3.171,
     'L0_gnn_b_hh': 5.189,
     'L0_ffn_gate_w': 5.551,
     'L0_ffn_w1': 5.111,
     'L0_ffn_w2': 5.052,
     'L0_ffn_w3': 5.054}
    for name, (base, spread) in spreads.items():
        noise = np.random.default_rng([zlib.crc32(name.encode()), seed]).standard_normal(out[name].shape)
        drawn = base * np.exp(spread * noise) if base else spread * noise
        out[name] = jnp.asarray(drawn.astype(out[name].dtype))
    for name, factor in factors.items():
        out[name] = (out[name] * factor).astype(out[name].dtype)
    return out
```

```python
from contextlib import ExitStack

import concourse.bass as bass
from concourse import mybir

F32 = mybir.dt.float32
F32R = mybir.dt.float32r
BF16 = mybir.dt.bfloat16
I32 = mybir.dt.int32
U32 = mybir.dt.uint32
ACT = mybir.ActivationFunctionType
ALU = mybir.AluOpType
AX = mybir.AxisListType

P = 128
EPS = 1e-5
SLOPE = 0.2
DS = 1.0 / 256.0


def gnn_moe(nc, x, adj, W, a, w_ih, w_hh, b_ih, b_hh, gate_w, gate_b, w1, w2, w3, out, rows):
    N, F = x.shape
    T = N // P
    KB = F // P
    NE, _, HID = w1.shape
    HB = HID // P
    G3 = 3 * F
    VW = F + 2
    HC = 1024
    Q = N // HC
    MC = 512
    CPT = N // MC
    JB = MC // P
    CQ = HC // MC
    RW = F + 4
    SLOTS = (2 * N + NE * (P - 1)) // P
    WR = 3


    ctx = ExitStack()
    with ctx:
        def sem(name):
            return ctx.enter_context(nc.semaphore(name))

        def sb(name, shape, dt, stack=ctx):
            return stack.enter_context(nc.sbuf_tensor(name, shape, dt))

        bank = [ctx.enter_context(nc.psum_tensor(f"bank{i}", [P, 512], F32)) for i in range(6)]
        pT = [ctx.enter_context(nc.psum_tensor(f"pT{i}", [P, 2 * MC], BF16)) for i in range(2)]
        accp, accm, rzb, nb, tp, tp2 = bank

        ident = sb("ident", [P, P], F32)
        identb = sb("identb", [P, P], BF16)
        before = sb("before", [P, P], BF16)
        onesb = sb("onesb", [P, P], BF16)
        iota_e = sb("iota_e", [P, NE], F32)
        pick = sb("pick", [P, 2, T, NE], BF16)
        gbias = sb("gbias", [P, NE], F32)
        gwt = sb("gwt", [P, KB, NE], F32)

        gs = ExitStack()
        V = sb("V", [P, T, 4, VW], F32R, gs)
        Dp = sb("Dp", [P, N], F32, gs)
        adjb = sb("adjb", [P, Q, HC], BF16, gs)
        gbuf = sb("gbuf", [P, HC], BF16, gs)
        tbuf = sb("tbuf", [P, 2, HC], BF16, gs)
        mask = sb("mask", [P, 2, 2, MC], F32R, gs)
        wT = sb("wT", [P, 2, KB, G3], F32, gs)
        xin = sb("xin", [P, 4, F], F32, gs)
        xnb = sb("xnb", [P, 2, F], F32, gs)
        hT = sb("hT", [P, 2 * KB, P], F32, gs)
        scr = sb("scr", [P, 6 * F], F32, gs)
        whs = sb("whs", [P, 2, VW], F32, gs)
        comb = sb("comb", [P, VW], F32, gs)
        xrow = sb("xrow", [P, 2, RW], F32, gs)
        xn2T = sb("xn2T", [P, KB, P], F32, gs)
        bias_rz = sb("bias_rz", [P, 2 * F], F32, gs)
        bias_n = sb("bias_n", [P, 2 * F], F32, gs)
        mean = sb("mean", [P, T], F32, gs)
        rstd = sb("rstd", [P, T], F32, gs)
        thr = sb("thr", [P, T], F32, gs)
        dcol = sb("dcol", [P, 2], F32, gs)
        BD = sb("BD", [P, T, 2], F32, gs)
        bst = sb("bst", [P, 6], F32, gs)
        mv = sb("mv", [P, 2], F32, gs)
        dmx = sb("dmx", [P, 2, Q], F32, gs)
        co = sb("co", [P, 2, 6], F32, gs)
        rden = sb("rden", [P, 1], F32, gs)
        var = sb("var", [P, 1], F32, gs)
        rs = sb("rs", [P, 1], F32, gs)
        mhalf = sb("mhalf", [P, 1], F32, gs)
        lg = sb("lg", [P, NE], F32, gs)
        top = sb("top", [P, 8], F32, gs)
        tix = sb("tix", [P, 8], U32, gs)
        rt = sb("rt", [P, 3], F32, gs)
        rz = scr[:, 0:2 * F]
        nn = scr[:, 2 * F:4 * F]
        hp = scr[:, 4 * F:5 * F]
        dd = scr[:, 5 * F:6 * F]
        wnat = scr[:, :].rearrange("p (r f) -> p r f", f=F)
        Wx = xrow[:, :, 0:VW]
        x1 = xin[:, 2, :]
        a_row = bias_rz[:, :]
        bhh_rz = xin[:, 2:4, :].rearrange("p a f -> p (a f)")
        gs.close()

        fs = ExitStack()
        wexp = sb("wexp", [P, WR, 3, KB * HID], F32, fs)
        xg = sb("xg", [P, WR, RW], F32, fs)
        xT = sb("xT", [P, WR, KB, P], F32, fs)
        sil = sb("sil", [P, HID], F32, fs)
        hid = sb("hid", [P, HID], F32, fs)
        hidT = sb("hidT", [P, HB, P], F32, fs)
        ysc = sb("ysc", [P, WR, F], F32, fs)
        lanew = sb("lanew", [P, WR, 2], F32, fs)
        iota_q = sb("iota_q", [P, P], F32, fs)
        cnt = sb("cnt", [P, NE, T], F32, fs)
        scan = sb("scan", [P, NE, T], F32, fs)
        ones = sb("ones", [P, NE, T], F32, fs)
        posw = sb("posw", [P, T, NE], F32, fs)
        prod = sb("prod", [P, 2, T, NE], F32, fs)
        pos = sb("pos", [P, 2, T], F32, fs)
        posi = sb("posi", [P, 2, T], I32, fs)
        poss = sb("poss", [P, 2, T], I32, fs)
        sidx = sb("sidx", [P, 2, T], F32, fs)
        qidx = sb("qidx", [P, 2, T], F32, fs)
        tok = sb("tok", [P, T], F32, fs)
        r16 = sb("r16", [P, 8, NE], F32, fs)
        kio = sb("kio", [P, T], F32, fs)
        cmp1 = sb("cmp1", [P, NE, T], F32, fs)
        sio = sb("sio", [P, SLOTS], F32, fs)
        cmp2 = sb("cmp2", [P, SLOTS, NE], F32, fs)
        esl = sb("esl", [P, SLOTS], F32, fs)
        esc = sb("esc", [P, SLOTS], F32, fs)
        esi = sb("esi", [P, SLOTS], I32, fs)
        sv = sb("sv", [P, SLOTS], F32, fs)
        gidx = sb("gidx", [P, SLOTS], U32, fs)
        cidx = sb("cidx", [P, SLOTS], U32, fs)
        gi1 = sb("gi1", [P, WR, 1], U32, fs)
        ci1 = sb("ci1", [P, WR, 1], U32, fs)
        lane_hot = sb("lane_hot", [P, 4, P], F32, fs)
        slot_hot = sb("slot_hot", [P, 4, SLOTS], F32, fs)
        fs.close()

        s_const = sem("constants_made")
        s_cld = sem("small_inputs_loaded")
        s_bld = sem("biases_loaded")
        s_wn = sem("gru_weights_loaded")
        s_wtr = sem("gru_weights_transposed")
        s_wev = sem("gru_weights_copied")
        s_wx = sem("W_extended")
        s_x = [sem(f"x_loaded{r}") for r in range(4)]
        s_var1 = sem("variance_of_x_done")
        s_rs1 = sem("deviation_of_x_done")
        s_var2 = sem("variance_of_x1_done")
        s_rs2 = sem("deviation_of_x1_done")
        s_xn = sem("xn_made")
        s_xt = sem("xn_transposed")
        s_xe = sem("xnT_copied")
        s_wh = sem("Wh_done")
        s_ws = sem("Wh_copied")
        s_bd = sem("value_scales_done")
        s_hi = sem("value_hi_done")
        s_lo = sem("value_lo_done")
        s_dc = sem("logit_columns_done")
        s_db = sem("d_broadcast")
        s_dpe = sem("d_broadcast_copied")
        s_vh = sem("denominator_hi_done")
        s_vd = sem("values_complete")
        s_link = sem("dve_link")
        s_adj = [sem(f"adj_loaded{q}") for q in range(Q)]
        s_t = sem("signed_adj_done")
        s_tr = sem("adj_transposed")
        s_mask = sem("masks_done")
        s_mm = sem("chunk_accumulated")
        s_nmx = sem("row_max_done")
        s_co = sem("row_scales_done")
        s_af = sem("accumulators_read")
        s_hp = sem("h_prime_done")
        s_xb = sem("xn_remade")
        s_th = sem("h_transposed")
        s_hT = sem("hT_copied")
        s_gru = sem("gru_products_done")
        s_rz = sem("rz_logits_done")
        s_gf = sem("gru_products_read")
        s_rzt = sem("rz_tanh_done")
        s_np = sem("n_logits_done")
        s_nt = sem("n_tanh_done")
        s_x1 = sem("x1_done")
        s_x1s = sem("x1_stored")
        s_xr = [sem(f"x_reloaded{u}") for u in range(2)]
        s_ln2 = sem("xn2_done")
        s_t2 = sem("xn2_transposed")
        s_t2e = sem("xn2T_copied")
        s_lgt = sem("gate_products_done")
        s_lg = sem("gate_logits_done")
        s_dl = sem("gate_difference_done")
        s_de = sem("gate_exp_done")
        s_row = sem("token_row_done")
        s_rows = [sem(f"token_row_stored{u}") for u in range(2)]
        s_rk = sem("ranks_done")
        s_io = sem("iotas_done")
        s_hot = sem("pair_one_hots_done")
        s_pl = sem("pair_placed")
        s_rd = sem("routing_done")
        s_w = [sem(f"expert_weights_loaded{r}") for r in range(WR)]
        s_gc = sem("gather_index_copied")
        s_cc = sem("scatter_index_copied")
        s_g = [sem(f"tokens_gathered{r}") for r in range(WR)]
        s_sc = sem("outputs_added")
        s_lw = sem("lane_weights_done")
        s_ftx = sem("slot_tokens_transposed")
        s_fxe = sem("slot_tokensT_copied")
        s_fh = sem("up_products_done")
        s_fs = sem("silu_done")
        s_fm = sem("hidden_done")
        s_fth = sem("hidden_transposed")
        s_fte = sem("hiddenT_copied")
        s_fy = sem("expert_outputs_done")
        s_fo = sem("weighted_outputs_done")

        block = ctx.enter_context(nc.Block())

        def tile_iterations(eng, body):
            for r in range(4):
                body(r, r, 0, r)
            with eng.Fori(1, T // 4 - 1) as g:
                for r in range(4):
                    body(g * 4 + r, r, g, None)
            for r in range(4):
                body(T - 4 + r, r, T // 4 - 1, T - 4 + r)

        LAST = T + 3
        L0 = 4
        NL = (T - 1 - L0) // 2
        L1 = L0 + 2 * NL

        def graph_iterations(eng, body):
            for i in range(L0):
                body(i, i % 2, i // 2, i)
            with eng.Fori(0, NL) as m:
                for n in range(2):
                    body(m * 2 + (L0 + n), (L0 + n) % 2, m + (L0 + n) // 2, None)
            for i in range(L1, LAST):
                body(i, i % 2, i // 2, i)

        def live(static, lag):
            return static is None or 0 <= static - lag < T

        def after(static, lag, n):
            return static is None or static - lag >= n

        FULL = (SLOTS - 2) // WR

        def slot_iterations(eng, body):
            for s in range(2 * WR):
                body(s, s % WR, s // WR, s)
            with eng.Fori(2, FULL) as m:
                for r in range(WR):
                    body(m * WR + r, r, m, None)
            for s in range(FULL * WR, SLOTS + 1):
                body(s, s % WR, s // WR, s)

        def at(t, size=1):
            return slice(t, t + size) if isinstance(t, int) else bass.ds(t, size)

        def wait_apart(eng, *waits):
            held = [(semaphore, v if isinstance(v, int) else eng.to_reg(v)) for semaphore, v in waits]
            eng.wait_ge(s_const, CONSTS)
            for semaphore, v in held:
                eng.wait_ge(semaphore, v)

        CONSTS = 9
        @block.sync
        def _(sp):
            row = lambda b, lo, hi: b[lo:hi].rearrange("(o f) -> o f", o=1).broadcast_to([P, hi - lo])
            sp.dma_start(Wx[:, :, 0:F], W.rearrange("(k p) f -> p k f", p=P)).then_inc(s_cld, 16)
            sp.dma_start(a_row, a.rearrange("f o -> o f").broadcast_to([P, 2 * F])).then_inc(s_cld, 16)
            sp.dma_start(gwt[:, :, :], gate_w.rearrange("(k p) e -> p k e", p=P)).then_inc(s_cld, 16)
            sp.dma_start(gbias[:, :], row(gate_b, 0, NE)).then_inc(s_cld, 16)
            for r in range(4):
                sp.dma_start(xin[:, r, :], x[r * P:(r + 1) * P, :]).then_inc(s_x[r], 16)
            sp.dma_start(wnat, w_ih.rearrange("(r p) f -> p r f", p=P)).then_inc(s_wn, 16)
            with sp.Fori(1, T // 4) as g:
                for r in range(4):
                    sp.wait_ge(s_xn, g * 4 + (r - 3))
                    sp.dma_start(xin[:, r, :], x[bass.ds((g * 4 + r) * P, P), :]).then_inc(s_x[r], 16)
            sp.wait_ge(s_wtr, 2 * KB)
            sp.dma_start(wnat, w_hh.rearrange("(r p) f -> p r f", p=P)).then_inc(s_wn, 16)
            sp.wait_ge(s_wx, 2 * KB)
            sp.dma_start(bias_rz[:, :], row(b_ih, 0, 2 * F)).then_inc(s_bld, 16)
            sp.dma_start(bias_n[:, 0:F], row(b_ih, 2 * F, 3 * F)).then_inc(s_bld, 16)
            sp.dma_start(bias_n[:, F:2 * F], row(b_hh, 2 * F, 3 * F)).then_inc(s_bld, 16)
            sp.wait_ge(s_xn, T)
            sp.dma_start(bhh_rz, row(b_hh, 0, 2 * F)).then_inc(s_bld, 16)

            def body(i, u, h, st):
                if live(st, 1):
                    if after(st, 1, 2):
                        sp.wait_ge(s_x1, i - 2)
                    sp.dma_start(xin[:, (u + 1) % 2, :], x[at((i - 1) * P, P), :]).then_inc(s_xr[(u + 1) % 2], 16)
                if live(st, 2):
                    sp.wait_ge(s_x1, i - 1)
                    sp.dma_start(out[at((i - 2) * P, P), :], x1).then_inc(s_x1s, 16)
                if live(st, 3):
                    sp.wait_ge(s_row, i - 2)
                    sp.dma_start(rows[at((i - 3) * P, P), :], xrow[:, (u + 1) % 2, :]).then_inc(s_rows[(u + 1) % 2], 16)

            graph_iterations(sp, body)

            w1v, w2v = (w.rearrange("e (p k) h -> e p (k h)", k=KB) for w in (w1, w2))
            w3v = w3.rearrange("e (p k) o -> e p (k o)", k=HB)
            sp.wait_ge(s_rd, 3)

            def load(s, r, m, st):
                if st == SLOTS:
                    return
                if st is None or st >= WR:
                    sp.wait_ge(s_fy, s - (WR - 1))
                e = sp.value_load(esi[0:1, at(s)], min_val=0, max_val=NE - 1)
                for n, wv in enumerate((w1v, w2v, w3v)):
                    sp.dma_start(wexp[:, r, n, :], wv[bass.ds(e, 1), :, :].rearrange("o p f -> (o p) f"))\
                      .then_inc(s_w[r], 16)

            slot_iterations(sp, load)
            sp.wait_ge(s_sc, 16 * SLOTS)

        @block.gpsimd
        def _(pool):
            def load_adj(t, q):
                pool.dma_start(adjb[:, q, :], adj[at(t * P, P), q * HC:(q + 1) * HC]).then_inc(s_adj[q], 16)

            nc.gpsimd.memset(ident[:], 0.0).then_inc(s_const, 1)
            nc.gpsimd.memset(before[:], 1.0).then_inc(s_const, 1)
            nc.gpsimd.memset(onesb[:], 1.0).then_inc(s_const, 1)
            nc.gpsimd.memset(mhalf[:], -0.5).then_inc(s_const, 1)
            nc.gpsimd.memset(V[:, :, :, F + 1:F + 2].bitcast(F32), 0.0).then_inc(s_const, 1)
            nc.gpsimd.iota(iota_e[:], [[1, NE]], base=0, channel_multiplier=0,
                           allow_small_or_imprecise_dtypes=True).then_inc(s_const, 1)
            pool.wait_ge(s_const, 6)
            nc.gpsimd.affine_select(out=ident[:], in_=ident[:], compare_op=ALU.not_equal, fill=1.0, base=0,
                                    pattern=[[-1, P]], channel_multiplier=1).then_inc(s_const, 1)
            nc.gpsimd.affine_select(out=before[:], in_=before[:], compare_op=ALU.is_gt, fill=0.0, base=0,
                                    pattern=[[1, P]], channel_multiplier=-1).then_inc(s_const, 1)
            pool.wait_ge(s_const, 8)
            nc.gpsimd.tensor_copy(identb[:], ident[:]).then_inc(s_const, 1)
            for q in range(Q):
                load_adj(0, q)

            def deviation(j, r, g, st):
                pool.wait_ge(s_var1, j + 1)
                nc.gpsimd.tensor_tensor(rs[:, :], var[:, :], mhalf[:, :], ALU.pow).then_inc(s_rs1, 1)

            tile_iterations(pool, deviation)

            def body(i, u, h, st):
                if st is None or st + 1 < T:
                    for q in range(Q):
                        pool.wait_ge(s_t, i * Q + (q + 1))
                        load_adj(i + 1, q)
                if live(st, 2):
                    pool.wait_ge(s_var2, i - 1)
                    nc.gpsimd.tensor_tensor(rs[:, :], var[:, :], mhalf[:, :], ALU.pow).then_inc(s_rs2, 1)

            graph_iterations(pool, body)

            pool.wait_ge(s_row, T)
            for par in range(2):
                pool.wait_ge(s_rows[par], 16 * (T // 2))
            pool.wait_ge(s_x1s, 16 * T)
            imp = dict(allow_small_or_imprecise_dtypes=True)
            nc.gpsimd.iota(sio[:], [[1, SLOTS]], base=0, channel_multiplier=0, **imp).then_inc(s_io, 1)
            nc.gpsimd.iota(kio[:], [[P, T]], base=0, channel_multiplier=0, **imp).then_inc(s_io, 1)
            nc.gpsimd.iota(iota_q[:], [[1, P]], base=0, channel_multiplier=0, **imp).then_inc(s_io, 1)
            nc.gpsimd.iota(tok[:], [[P, T]], base=1, channel_multiplier=1, **imp).then_inc(s_io, 1)
            nc.gpsimd.memset(ones[:], 1.0).then_inc(s_io, 1)

            def gather(s, r, m, st):
                if st is None or st >= WR:
                    pool.wait_ge(s_lw, s - (WR - 1))
                    pool.wait_ge(s_ftx, s - (WR - 1))
                nc.gpsimd.tensor_copy(gi1[:, r, :], gidx[:, at(s)]).then_inc(s_gc, 1)
                wait_apart(pool, (s_gc, s + 1))
                nc.gpsimd.indirect_dma_start(
                    out=xg[:, r, :], out_offset=None, in_=rows[:, :],
                    in_offset=bass.IndirectOffsetOnAxis(ap=gi1[:, r, :], axis=0)).then_inc(s_g[r], 16)

            def scatter(s, r, m, st):
                nc.gpsimd.tensor_copy(ci1[:, r, :], cidx[:, at(s)]).then_inc(s_cc, 1)
                waits = [(s_cc, s + 1), (s_fo, s + 1)]
                if st is None or st >= 1:
                    waits.append((s_sc, s * 16))
                wait_apart(pool, *waits)
                nc.gpsimd.indirect_dma_start(
                    out=out[:, :], out_offset=bass.IndirectOffsetOnAxis(ap=ci1[:, r, :], axis=0),
                    in_=ysc[:, r, :], in_offset=None, compute_op=ALU.add,
                    bounds_check=N - 1, oob_is_err=False).then_inc(s_sc, 16)

            pool.wait_ge(s_rd, 3)
            gather(0, 0, 0, 0)
            gather(1, 1, 0, 1)

            def slot(s, r, m, st):
                if st is None or st + 2 < SLOTS:
                    gather(s + 2, (r + 2) % WR, m + (r + 2) // WR, None if st is None else st + 2)
                if st is None or st >= 1:
                    scatter(s - 1, (r - 1) % WR, m + (r - 1) // WR, None if st is None else st - 1)

            slot_iterations(pool, slot)

        @block.scalar
        def _(act):
            act_copy = lambda o, i: nc.scalar.activation(o, i, ACT.Copy)

            def copy_gru_weights(m):
                for n in range(2 * KB):
                    kb, half = n // 2, n % 2
                    act.wait_ge(s_wtr, 2 * KB * m + n + 1)
                    act_copy(wT[:, m, kb, half * 3 * P:(half + 1) * 3 * P],
                             (accp, accm)[n % 2][:, 0:3 * P]).then_inc(s_wev, 1)

            copy_gru_weights(0)

            def copy_xT(j, r, st):
                act.wait_ge(s_xt, j + 1)
                if st is None or st >= 2:
                    act.wait_ge(s_wh, j - 1)
                p = r % 2
                act_copy(hT[:, KB * p:KB * p + KB, :].rearrange("p k m -> p (k m)"),
                         (tp, tp2)[p][:, 0:F]).then_inc(s_xe, 1)

            copy_xT(0, 0, 0)

            def values(j, r, g, st):
                if st is None or st + 1 < T:
                    copy_xT(j + 1, r + 1, None if st is None else st + 1)
                wh = whs[:, r % 2, :]
                act.wait_ge(s_wh, j + 1)
                if st is None or st >= 2:
                    act.wait_ge(s_lo, (j - 1) * 2)
                act_copy(wh, (rzb, nb)[r % 2][:, 0:VW]).then_inc(s_ws, 1)
                act.wait_ge(s_ws, j + 1)
                for k, slope in enumerate((1.0, SLOPE)):
                    nc.scalar.activation(BD[:, at(j), k], wh[:, F:F + 1], ACT.Exp, scale=slope).then_inc(s_bd, 1)
                for k in range(2):
                    act.wait_ge(s_bd, j * 2 + (k + 1))
                    nc.scalar.activation(V[:, at(j), 2 * k, 0:F], wh[:, 0:F], ACT.Copy,
                                         scale=BD[:, at(j), k]).then_inc(s_hi, 1)
                act.wait_ge(s_db, j + 1)
                act_copy(Dp[:, at(j * P, P)], (accp, accm)[r % 2][:, 0:P]).then_inc(s_dpe, 1)

            tile_iterations(act, values)
            for k in range(2):
                act_copy(V[:, :, 2 * k, F], BD[:, :, k]).then_inc(s_vh, 1)
            copy_gru_weights(1)

            def masks(i, c, st):
                C = i * CPT + c
                act.wait_ge(s_tr, C + 1)
                if st is None or st * CPT + c >= 2:
                    act.wait_ge(s_mm, C - 1)
                for k, sign in enumerate((2.0, -2.0)):
                    ins = nc.scalar.activation(mask[:, c % 2, k, :], pT[c % 2][:, 0:MC], ACT.Relu, scale=sign)
                ins.then_inc(s_mask, 1)

            masks(0, 0, 0)

            def rz_tanh(i, u):
                act.wait_ge(s_rz, i - 1)
                nc.scalar.activation(rz, rz, ACT.Tanh, scale=0.5).then_inc(s_rzt, 1)

            def n_tanh(i, u):
                act.wait_ge(s_np, i - 1)
                nc.scalar.activation(nn[:, 0:F], nn[:, 0:F], ACT.Tanh).then_inc(s_nt, 1)

            def copy_hT(i, u, st):
                act.wait_ge(s_th, i)
                if after(st, 1, 1):
                    act.wait_ge(s_gru, i - 1)
                act_copy(hT[:, :, :].rearrange("p k m -> p (k m)"), tp[:, :]).then_inc(s_hT, 1)

            def gate_exp(i, u):
                act.wait_ge(s_dl, i - 2)
                nc.scalar.activation(rt[:, 1:2], rt[:, 0:1], ACT.Exp).then_inc(s_de, 1)

            def row_scales(i, u):
                act.wait_ge(s_nmx, i + 1)
                for k, slope in enumerate((1.0, SLOPE)):
                    ins = nc.scalar.activation(co[:, u, k:k + 1], thr[:, at(i)], ACT.Exp, scale=-slope / DS,
                                               bias=co[:, u, 5:6])
                ins.then_inc(s_co, 1)

            def body(i, u, h, st):
                if live(st, 3):
                    act.wait_ge(s_t2, i - 2)
                    act_copy(xn2T[:, :, :].rearrange("p k m -> p (k m)"), tp2[:, 0:F]).then_inc(s_t2e, 1)
                for c in range(CPT):
                    if c and live(st, 0):
                        masks(i, c, st)
                    if c == 1 and live(st, 2):
                        rz_tanh(i, u)
                    if c == min(3, CPT - 1) and live(st, 1):
                        copy_hT(i, u, st)
                    if c == min(4, CPT - 1):
                        if live(st, 2):
                            n_tanh(i, u)
                        if live(st, 3):
                            gate_exp(i, u)
                    if c == min(6, CPT - 1) and live(st, 0):
                        row_scales(i, u)
                if st is None or st + 1 < T:
                    masks(i + 1, 0, None if st is None else st + 1)

            graph_iterations(act, body)

            def copy_slot_xT(s, r, st):
                act.wait_ge(s_ftx, s + 1)
                if st is None or st >= WR:
                    act.wait_ge(s_fh, (s - (WR - 1)) * 2)
                act_copy(xT[:, r, :, :].rearrange("p k m -> p (k m)"), tp[:, 0:F]).then_inc(s_fxe, 1)

            copy_slot_xT(0, 0, 0)

            def slot(s, r, m, st):
                if st == SLOTS:
                    return
                act.wait_ge(s_fh, s * 2 + 1)
                if st is None or st >= 1:
                    act.wait_ge(s_fm, s)
                nc.scalar.activation(sil[:, :], rzb[:, :], ACT.Silu).then_inc(s_fs, 1)
                if st is None or st + 1 < SLOTS:
                    copy_slot_xT(s + 1, (r + 1) % WR, None if st is None else st + 1)
                act.wait_ge(s_fth, s + 1)
                if st is None or st >= 1:
                    act.wait_ge(s_fy, s)
                act_copy(hidT[:, :, :].rearrange("p k m -> p (k m)"), tp2[:, :]).then_inc(s_fte, 1)

            slot_iterations(act, slot)

        @block.vector
        def _(dve):
            V_ = nc.vector
            done = [0]

            def link(ins, alone=False):
                done[0] = done[0] + 1
                ins.then_inc(s_link, 1)
                if alone:
                    wait_apart(dve, (s_link, done[0]))
                else:
                    dve.wait_ge(s_link, done[0])

            dve.wait_ge(s_cld, 64)
            for kb in range(KB):
                for n in range(2):
                    half = a_row[:, F:2 * F] if n == 0 else a_row[:, 0:F]
                    V_.tensor_tensor_reduce(out=comb[:, 0:F], in0=Wx[:, kb, 0:F], in1=half, scale=1.0, scalar=0.0, op0=ALU.mult,
                                            op1=ALU.add, accum_out=Wx[:, kb, F + n:F + n + 1]).then_inc(s_wx, 1)
                    dve.wait_ge(s_wx, 2 * kb + n + 1)

            def moments(src, var_done):
                link(V_.bn_stats(bst[:, :], src), True)
                link(V_.bn_aggr(mv[:, :], bst[:, :]))
                V_.tensor_scalar(var[:, :], mv[:, 1:2], EPS, None, ALU.add).then_inc(var_done, 1)

            def layernorm(j, r, g, st):
                dve.wait_ge(s_x[r], g * 16 + 16)
                src = xin[:, r, :]
                moments(src, s_var1)
                link(V_.tensor_copy(mean[:, at(j)], mv[:, 0:1]))
                dve.wait_ge(s_rs1, j + 1)
                V_.tensor_copy(rstd[:, at(j)], rs[:, :])
                if st is None or st >= 2:
                    dve.wait_ge(s_xt, j - 1)
                V_.tensor_scalar(xnb[:, r % 2, :], src, mv[:, 0:1], rs[:, 0:1], ALU.subtract,
                                 ALU.mult).then_inc(s_xn, 1)

            layernorm(0, 0, 0, 0)
            LN_LINKS = 3

            def values(j, r, g, st):
                done[0] = j * LN_LINKS + LN_LINKS
                if st is None or st + 1 < T:
                    layernorm(j + 1, (r + 1) % 4, g + (r + 1) // 4, None if st is None else st + 1)
                wh = whs[:, r % 2, :]
                dve.wait_ge(s_ws, j + 1)
                if st is None or st >= 2:
                    dve.wait_ge(s_db, j - 1)
                V_.tensor_scalar(dcol[:, r % 2:r % 2 + 1], wh[:, F:F + 1], DS, None, ALU.mult).then_inc(s_dc, 1)
                V_.tensor_scalar(thr[:, at(j)], wh[:, F + 1:F + 2], -DS, None, ALU.mult)
                for k in range(2):
                    dve.wait_ge(s_hi, j * 2 + (k + 1))
                    V_.scalar_tensor_tensor(out=V[:, at(j), 2 * k + 1, 0:F], in0=wh[:, 0:F], scalar=BD[:, at(j), k],
                                            in1=V[:, at(j), 2 * k, 0:F].bitcast(F32), op0=ALU.mult,
                                            op1=ALU.subtract).then_inc(s_lo, 1)

            tile_iterations(dve, values)
            assert done[0] == T * LN_LINKS
            for k in range(2):
                dve.wait_ge(s_vh, k + 1)
                V_.tensor_tensor(V[:, :, 2 * k + 1, F], BD[:, :, k], V[:, :, 2 * k, F].bitcast(F32),
                                 ALU.subtract).then_inc(s_vd, 1)
            dve.wait_ge(s_bld, 64)
            link(V_.tensor_tensor(bias_rz[:, :], bias_rz[:, :], bhh_rz, ALU.add))
            dve.wait_ge(s_dpe, T)

            def piece(i, q, u, st):
                waits = [(s_adj[q], i * 16 + 16)]
                if st is None or st or q:
                    waits.append((s_t, i * Q + q))
                wait_apart(dve, *waits)
                cols = slice(q * HC, (q + 1) * HC)
                link(V_.tensor_tensor_reduce(out=gbuf[:, :], in0=Dp[:, cols], in1=adjb[:, q, :], scale=1.0, scalar=-1e30,
                                             op0=ALU.add, op1=ALU.max, accum_out=dmx[:, u, q:q + 1]))
                link(V_.tensor_scalar(gbuf[:, :], Dp[:, cols], thr[:, at(i)], 0.5, ALU.is_gt, ALU.subtract))
                if st is None or st * Q + q >= 2:
                    dve.wait_ge(s_tr, (i * Q + (q - 1)) * CQ)
                V_.tensor_tensor(tbuf[:, q % 2, :], adjb[:, q, :], gbuf[:, :], ALU.mult).then_inc(s_t, 1)

            def row_max(i, u):
                c = lambda k: co[:, u, k:k + 1]
                link(V_.tensor_reduce(c(2), dmx[:, u, :], AX.X, ALU.max))
                link(V_.tensor_scalar(c(3), c(2), 1.0, thr[:, at(i)], ALU.subtract, ALU.subtract))
                link(V_.tensor_scalar(c(4), c(3), -SLOPE / DS, None, ALU.mult))
                V_.scalar_tensor_tensor(out=c(5), in0=c(3), scalar=-1.0 / DS, in1=c(4), op0=ALU.mult,
                                        op1=ALU.min).then_inc(s_nmx, 1)

            def combine(i, u, st):
                v = (u + 1) % 2
                dve.wait_ge(s_mm, i * CPT)
                dve.wait_ge(s_co, i)
                link(V_.tensor_scalar(comb[:, 0:F + 1], accm[:, 0:F + 1], co[:, v, 1:2], None, ALU.mult))
                V_.scalar_tensor_tensor(out=comb[:, 0:F + 1], in0=accp[:, 0:F + 1], scalar=co[:, v, 0:1],
                                        in1=comb[:, 0:F + 1], op0=ALU.mult, op1=ALU.add).then_inc(s_af, 1)
                dve.wait_ge(s_af, i)
                link(V_.reciprocal(rden[:, :], comb[:, F:F + 1]))
                if after(st, 1, 1):
                    dve.wait_ge(s_th, i - 1)
                V_.tensor_scalar(hp, comb[:, 0:F], rden[:, 0:1], None, ALU.mult).then_inc(s_hp, 1)

            def remake_xn(i, u, h, st):
                v = (u + 1) % 2
                dve.wait_ge(s_xr[v], (h + (u - 1) // 2) * 16 + 16)
                V_.tensor_scalar(xnb[:, v, :], xin[:, v, :], mean[:, at(i - 1)], rstd[:, at(i - 1)], ALU.subtract,
                                 ALU.mult).then_inc(s_xb, 1)

            def gru_logits(i):
                dve.wait_ge(s_gru, i - 1)
                V_.tensor_tensor(rz, rzb[:, :], bias_rz[:, :], ALU.add).then_inc(s_rz, 1)
                V_.tensor_tensor(nn, nb[:, :], bias_n[:, :], ALU.add).then_inc(s_gf, 1)

            def gru_n(i):
                dve.wait_ge(s_rzt, i - 1)
                dve.wait_ge(s_gf, i - 1)
                link(V_.scalar_tensor_tensor(out=nn[:, F:2 * F], in0=rz[:, 0:F], scalar=1.0, in1=nn[:, F:2 * F],
                                             op0=ALU.add, op1=ALU.mult))
                V_.scalar_tensor_tensor(out=nn[:, 0:F], in0=nn[:, F:2 * F], scalar=0.5, in1=nn[:, 0:F], op0=ALU.mult,
                                        op1=ALU.add).then_inc(s_np, 1)

            def gru_out(i, u, st):
                dve.wait_ge(s_nt, i - 1)
                link(V_.tensor_tensor(dd, xnb[:, u, :], nn[:, 0:F], ALU.subtract))
                link(V_.scalar_tensor_tensor(out=dd, in0=rz[:, F:2 * F], scalar=1.0, in1=dd, op0=ALU.add, op1=ALU.mult))
                link(V_.scalar_tensor_tensor(out=dd, in0=dd, scalar=0.5, in1=nn[:, 0:F], op0=ALU.mult, op1=ALU.add))
                if after(st, 2, 1):
                    dve.wait_ge(s_x1s, (i - 2) * 16)
                V_.tensor_tensor(x1, dd, xin[:, u, :], ALU.add).then_inc(s_x1, 1)

            def norm2(i, u, h, st):
                dve.wait_ge(s_x1, i - 1)
                moments(x1, s_var2)
                dve.wait_ge(s_rs2, i - 1)
                if after(st, 2, 2):
                    dve.wait_ge(s_rows[u], (h + (u - 4) // 2) * 16 + 16)
                V_.tensor_scalar(xrow[:, u, 0:F], x1, mv[:, 0:1], rs[:, 0:1], ALU.subtract, ALU.mult).then_inc(s_ln2, 1)

            def route_top(i, u):
                v = (u + 1) % 2
                dve.wait_ge(s_lgt, i - 2)
                V_.tensor_tensor(lg[:, :], tp2[:, F:F + NE], gbias[:, :], ALU.add).then_inc(s_lg, 1)
                wait_apart(dve, (s_lg, i - 2))
                link(V_.max(top[:, :], lg[:, :]))
                V_.tensor_tensor(rt[:, 0:1], top[:, 1:2], top[:, 0:1], ALU.subtract).then_inc(s_dl, 1)
                link(V_.max_index(tix[:, :], top[:, :], lg[:, :]))
                link(V_.tensor_copy(xrow[:, v, F + 2:F + 4], tix[:, 0:2]))
                for k in range(2):
                    V_.tensor_scalar(pick[:, k, at(i - 3), :], iota_e[:, :], xrow[:, v, F + 2 + k:F + 3 + k], None,
                                     ALU.is_equal)

            def route_weights(i, u):
                v = (u + 1) % 2
                dve.wait_ge(s_de, i - 2)
                link(V_.tensor_scalar(rt[:, 2:3], rt[:, 1:2], 1.0, None, ALU.add))
                link(V_.reciprocal(xrow[:, v, F:F + 1], rt[:, 2:3]))
                V_.tensor_tensor(xrow[:, v, F + 1:F + 2], rt[:, 1:2], xrow[:, v, F:F + 1], ALU.mult).then_inc(s_row, 1)

            piece(0, 0, 0, 0)
            loop_links = [None, None]
            ITER_LINKS = 2 * Q + 3 + 2 + 1 + 3 + 2 + 3 + 2

            def body(i, u, h, st):
                if st is None:
                    if loop_links[0] is None:
                        loop_links[0] = done[0]
                    done[0] = loop_links[0] + (i - L0) * ITER_LINKS
                elif loop_links[0] is not None and st == L1:
                    done[0] = loop_links[0] + (L1 - L0) * ITER_LINKS
                start = done[0]
                if live(st, 1):
                    combine(i, u, st)
                    remake_xn(i, u, h, st)
                if live(st, 0) and Q > 1:
                    piece(i, 1, u, st)
                if live(st, 2):
                    gru_logits(i)
                if live(st, 0) and Q > 2:
                    piece(i, 2, u, st)
                if live(st, 2):
                    gru_n(i)
                if live(st, 3):
                    route_top(i, u)
                if live(st, 0):
                    for q in range(3, Q):
                        piece(i, q, u, st)
                if live(st, 2):
                    gru_out(i, u, st)
                if live(st, 0):
                    row_max(i, u)
                if live(st, 3):
                    route_weights(i, u)
                if st is None or st + 1 < T:
                    piece(i + 1, 0, (u + 1) % 2, None if st is None else st + 1)
                if live(st, 2):
                    norm2(i, u, h, st)
                if st is not None and L0 <= st < T - 1:
                    assert done[0] - start == ITER_LINKS, (done[0] - start, ITER_LINKS)

            graph_iterations(dve, body)

            dve.wait_ge(s_rows[0], 16 * (T // 2))
            dve.wait_ge(s_rows[1], 16 * (T // 2))
            dve.wait_ge(s_x1s, 16 * T)
            dve.wait_ge(s_rk, 2)
            dve.wait_ge(s_io, 5)
            R = lambda k: r16[:, k, :]
            per_t = lambda v: v.unsqueeze(2).broadcast_to([P, NE, T])
            total, tiles, tend, tstart, tincl, estart, base = (R(k) for k in range(7))
            link(V_.tensor_copy(cnt[:, :, :], nb[:, 0:T * NE].rearrange("p (t e) -> p e t", e=NE)))
            link(V_.tensor_reduce(total, cnt[:, :, :], AX.X, ALU.add))
            flat = lambda v: v.rearrange("p e t -> p (e t)")
            link(V_.tensor_tensor_scan(flat(scan[:, :, :]), flat(ones[:, :, :]), flat(cnt[:, :, :]), 0.0, ALU.mult, ALU.add))
            link(V_.tensor_tensor(cmp1[:, :, :], per_t(total), kio[:, :].unsqueeze(1).broadcast_to([P, NE, T]), ALU.is_gt))
            link(V_.tensor_reduce(tiles, cmp1[:, :, :], AX.X, ALU.add))
            link(V_.tensor_tensor_scan(tend, ones[:, 0, 0:NE], tiles, 0.0, ALU.mult, ALU.add))
            link(V_.tensor_tensor_scan(tincl, ones[:, 0, 0:NE], total, 0.0, ALU.mult, ALU.add))
            link(V_.tensor_tensor(tstart, tend, tiles, ALU.subtract))
            link(V_.tensor_tensor(estart, tincl, total, ALU.subtract))
            link(V_.scalar_tensor_tensor(out=base, in0=tstart, scalar=float(P), in1=estart, op0=ALU.mult, op1=ALU.subtract))
            link(V_.tensor_tensor(cmp1[:, :, :], scan[:, :, :], cnt[:, :, :], ALU.subtract))
            link(V_.tensor_tensor(cmp1[:, :, :], cmp1[:, :, :], per_t(base), ALU.add))
            link(V_.tensor_tensor(posw[:, :, :].rearrange("p t e -> p e t"), cmp1[:, :, :],
                                  rzb[:, 0:T * NE].rearrange("p (t e) -> p e t", e=NE), ALU.add))
            for k in range(2):
                link(V_.tensor_tensor(prod[:, k, :, :], pick[:, k, :, :], posw[:, :, :], ALU.mult))
            link(V_.tensor_reduce(pos[:, :, :].rearrange("p k t -> p (k t)"),
                                  prod[:, :, :, :].rearrange("p k t e -> p (k t) e"), AX.X, ALU.add))
            link(V_.tensor_copy(posi[:, :, :], pos[:, :, :]))
            link(V_.tensor_single_scalar(poss[:, :, :], posi[:, :, :], P.bit_length() - 1, ALU.arith_shift_right))
            link(V_.tensor_copy(sidx[:, :, :], poss[:, :, :]))
            link(V_.scalar_tensor_tensor(out=qidx[:, :, :], in0=sidx[:, :, :], scalar=-float(P), in1=pos[:, :, :],
                                         op0=ALU.mult, op1=ALU.add))

            def pair(t, k, b, st):
                n = t * 2 + k
                if st is None or 2 * st + k >= 4:
                    dve.wait_ge(s_pl, n - 3)
                V_.tensor_scalar(lane_hot[:, b, :], iota_q[:, :], qidx[:, k, at(t)], None,
                                 ALU.is_equal).then_inc(s_hot, 1)
                V_.tensor_scalar(slot_hot[:, b, :], sio[:, :], sidx[:, k, at(t)], tok[:, at(t)], ALU.is_equal,
                                 ALU.mult).then_inc(s_hot, 1)

            for k in range(4):
                pair(k // 2, k % 2, k, k // 2)
            with dve.Fori(1, T // 2 - 1) as m:
                for k in range(4):
                    pair(m * 2 + k // 2, k % 2, k, None)
            for k in range(4):
                pair(T - 2 + k // 2, k % 2, k, T - 2 + k // 2)

            link(V_.tensor_tensor(cmp2[:, :, :], sio[:, :].unsqueeze(2).broadcast_to([P, SLOTS, NE]),
                                  tend.unsqueeze(1).broadcast_to([P, SLOTS, NE]), ALU.is_ge))
            link(V_.tensor_reduce(esc[:, :], cmp2[:, :, :], AX.X, ALU.add))
            link(V_.tensor_scalar(esl[:, :], esc[:, :], float(NE - 1), None, ALU.min))
            V_.tensor_copy(esi[:, :], esl[:, :]).then_inc(s_rd, 1)
            dve.wait_ge(s_pl, 2 * T)
            V_.tensor_scalar(gidx[:, :], accp[:, 0:SLOTS], -1.0, 0.0, ALU.add, ALU.max).then_inc(s_rd, 1)
            link(V_.tensor_scalar(sv[:, :], accp[:, 0:SLOTS], 0.0, float(2 * N), ALU.is_equal, ALU.mult))
            V_.scalar_tensor_tensor(out=cidx[:, :], in0=accp[:, 0:SLOTS], scalar=-1.0, in1=sv[:, :], op0=ALU.add,
                                    op1=ALU.add).then_inc(s_rd, 1)

            slot_base = done[0]
            SLOT_LINKS = 2

            def slot(s, r, m, st):
                done[0] = slot_base + s * SLOT_LINKS
                if st is None or st < SLOTS:
                    dve.wait_ge(s_g[r], m * 16 + 16)
                    if st is None or st >= WR:
                        dve.wait_ge(s_fo, s - (WR - 1))
                    e = esl[:, at(s)]
                    link(V_.tensor_scalar(lanew[:, r, 0:1], xg[:, r, F + 2:F + 3], e, xg[:, r, F:F + 1],
                                          ALU.is_equal, ALU.mult))
                    link(V_.tensor_scalar(lanew[:, r, 1:2], xg[:, r, F + 3:F + 4], e, xg[:, r, F + 1:F + 2],
                                          ALU.is_equal, ALU.mult))
                    V_.tensor_tensor(lanew[:, r, 0:1], lanew[:, r, 0:1], lanew[:, r, 1:2], ALU.add).then_inc(s_lw, 1)
                    dve.wait_ge(s_fs, s + 1)
                    dve.wait_ge(s_fh, s * 2 + 2)
                    if st is None or st >= 1:
                        dve.wait_ge(s_fth, s)
                    V_.tensor_tensor(hid[:, :], nb[:, :], sil[:, :], ALU.mult).then_inc(s_fm, 1)
                if st is None or st >= 1:
                    v = (r - 1) % WR
                    dve.wait_ge(s_fy, s)
                    dve.wait_ge(s_lw, s)
                    if st is None or st >= WR + 1:
                        dve.wait_ge(s_sc, (s - WR) * 16)
                    V_.tensor_scalar(ysc[:, v, :], accp[:, 0:F], lanew[:, v, 0:1], None, ALU.mult).then_inc(s_fo, 1)

            slot_iterations(dve, slot)

        @block.tensor
        def _(pe):
            mm = nc.tensor.matmul
            tr = lambda o, i: nc.tensor.transpose(o, i, ident[:, :])

            def transpose_gru_weights(m):
                pe.wait_ge(s_wn, 16 * (m + 1))
                for n in range(2 * KB):
                    kb, half = n // 2, n % 2
                    if m or n >= 2:
                        pe.wait_ge(s_wev, 2 * KB * m + n - 1)
                    for r in range(3):
                        ins = tr((accp, accm)[n % 2][:, r * P:(r + 1) * P],
                                 wnat[:, half * 3 + r, kb * P:(kb + 1) * P])
                    ins.then_inc(s_wtr, 1)

            pe.wait_ge(s_const, CONSTS)
            transpose_gru_weights(0)
            pe.wait_ge(s_wev, 2 * KB)

            def transpose_xn(j, r, st):
                pe.wait_ge(s_xn, j + 1)
                if st is None or st >= 2:
                    pe.wait_ge(s_xe, j - 1)
                p = r % 2
                for kb in range(KB):
                    ins = tr((tp, tp2)[p][:, kb * P:(kb + 1) * P], xnb[:, p, kb * P:(kb + 1) * P])
                ins.then_inc(s_xt, 1)

            transpose_xn(0, 0, 0)
            pe.wait_ge(s_wx, 2 * KB)

            def values(j, r, g, st):
                if st is None or st + 1 < T:
                    transpose_xn(j + 1, r + 1, None if st is None else st + 1)
                p = r % 2
                pe.wait_ge(s_xe, j + 1)
                if st is None or st >= 2:
                    pe.wait_ge(s_ws, j - 1)
                wh = (rzb, nb)[p]
                for kb in range(KB):
                    ins = mm(wh[:, 0:VW], hT[:, KB * p + kb, :], Wx[:, kb, :], start=kb == 0, stop=kb == KB - 1)
                ins.then_inc(s_wh, 1)
                pe.wait_ge(s_dc, j + 1)
                if st is None or st >= 2:
                    pe.wait_ge(s_dpe, j - 1)
                mm((accp, accm)[p][:, 0:P], dcol[:, p:p + 1].broadcast_to([P, P]), ident[:, :], start=True,
                   stop=True).then_inc(s_db, 1)

            tile_iterations(pe, values)
            pe.wait_ge(s_dpe, T)
            transpose_gru_weights(1)

            def transpose_adj(i, c, st):
                C = i * CPT + c
                q = c // CQ
                pe.wait_ge(s_t, i * Q + (q + 1))
                if st is None or st * CPT + c >= 2:
                    pe.wait_ge(s_mask, C - 1)
                for b in range(JB):
                    at0 = (c % CQ) * MC + b * P
                    ins = nc.tensor.transpose(pT[c % 2][:, b * P:(b + 1) * P], tbuf[:, q % 2, at0:at0 + P],
                                              identb[:, :])
                ins.then_inc(s_tr, 1)

            def accumulate(i, c, st):
                pe.wait_ge(s_mask, i * CPT + (c + 1))
                if c == 0 and after(st, 0, 1):
                    pe.wait_ge(s_af, i)
                for b in range(JB):
                    j = c * JB + b
                    for k, acc in enumerate((accp, accm)):
                        for part in range(2):
                            ins = mm(acc[:, 0:VW], mask[:, c % 2, k, b * P:(b + 1) * P], V[:, j, 2 * k + part, :],
                                     start=j == 0 and part == 0, stop=j == T - 1 and part == 1)
                ins.then_inc(s_mm, 1)

            def transpose_h(i, u, st):
                v = (u + 1) % 2
                pe.wait_ge(s_hp, i)
                pe.wait_ge(s_xb, i)
                if after(st, 1, 1):
                    pe.wait_ge(s_hT, i - 1)
                for n, src in enumerate((hp, xnb[:, v, :])):
                    for kb in range(KB):
                        ins = tr(tp[:, (n * KB + kb) * P:(n * KB + kb + 1) * P], src[:, kb * P:(kb + 1) * P])
                ins.then_inc(s_th, 1)

            def gru(i, st):
                pe.wait_ge(s_hT, i - 1)
                if after(st, 2, 1):
                    pe.wait_ge(s_gf, i - 2)
                for n in range(2 * KB):
                    mm(rzb[:, :], hT[:, n, :], wT[:, n // KB, n % KB, 0:2 * F], start=n == 0, stop=n == 2 * KB - 1)
                for n in range(2 * KB):
                    m, kb = n // KB, n % KB
                    ins = mm(nb[:, m * F:(m + 1) * F], hT[:, n, :], wT[:, m, kb, 2 * F:3 * F], start=kb == 0,
                             stop=kb == KB - 1)
                ins.then_inc(s_gru, 1)

            def transpose_x2(i, u, st):
                v = (u + 1) % 2
                pe.wait_ge(s_ln2, i - 2)
                if after(st, 3, 1):
                    pe.wait_ge(s_lg, i - 3)
                for kb in range(KB):
                    ins = tr(tp2[:, kb * P:(kb + 1) * P], xrow[:, v, kb * P:(kb + 1) * P])
                ins.then_inc(s_t2, 1)

            def gate(i):
                pe.wait_ge(s_t2e, i - 2)
                for kb in range(KB):
                    ins = mm(tp2[:, F:F + NE], xn2T[:, kb, :], gwt[:, kb, :], start=kb == 0, stop=kb == KB - 1)
                ins.then_inc(s_lgt, 1)

            pe.wait_ge(s_vd, 2)
            pe.wait_ge(s_lo, 2 * T)
            pe.wait_ge(s_wev, 4 * KB)
            transpose_adj(0, 0, 0)

            def body(i, u, h, st):
                if live(st, 3):
                    transpose_x2(i, u, st)
                if live(st, 2):
                    gru(i, st)
                if live(st, 3):
                    gate(i)
                for c in range(CPT):
                    if live(st, 0):
                        if c + 1 < CPT:
                            transpose_adj(i, c + 1, st)
                        elif st is None or st + 1 < T:
                            transpose_adj(i + 1, 0, None if st is None else st + 1)
                        accumulate(i, c, st)
                    if c == min(2, CPT - 1) and live(st, 1):
                        transpose_h(i, u, st)

            graph_iterations(pe, body)

            pe.wait_ge(s_row, T)
            for lhs, acc in ((before, rzb), (onesb, nb)):
                for k in range(2):
                    ins = mm(acc[:, 0:T * NE], lhs[:, :], pick[:, k, :, :].rearrange("p t e -> p (t e)"), start=k == 0,
                             stop=k == 1)
                ins.then_inc(s_rk, 1)

            def place(t, k, b, st):
                pe.wait_ge(s_hot, t * 4 + (2 * k + 2))
                mm(accp[:, 0:SLOTS], lane_hot[:, b, :], slot_hot[:, b, :], start=st == 0 and k == 0,
                   stop=st == T - 1 and k == 1).then_inc(s_pl, 1)

            for k in range(4):
                place(k // 2, k % 2, k, k // 2)
            with pe.Fori(1, T // 2 - 1) as m:
                for k in range(4):
                    place(m * 2 + k // 2, k % 2, k, None)
            for k in range(4):
                place(T - 2 + k // 2, k % 2, k, T - 2 + k // 2)

            def transpose_tokens(s, r, m, st):
                pe.wait_ge(s_g[r], m * 16 + 16)
                if st is None or st >= 1:
                    pe.wait_ge(s_fxe, s)
                for k in range(KB):
                    ins = tr(tp[:, k * P:(k + 1) * P], xg[:, r, k:F:KB])
                ins.then_inc(s_ftx, 1)

            transpose_tokens(0, 0, 0, 0)

            def slot(s, r, m, st):
                here = st is None or st < SLOTS
                if here:
                    pe.wait_ge(s_w[r], m * 48 + 48)
                    pe.wait_ge(s_fxe, s + 1)
                    for n, acc in enumerate((rzb, nb)):
                        if st is None or st >= 1:
                            pe.wait_ge((s_fs, s_fm)[n], s)
                        for k in range(KB):
                            ins = mm(acc[:, 0:HID], xT[:, r, k, :], wexp[:, r, n, k * HID:(k + 1) * HID],
                                     start=k == 0, stop=k == KB - 1)
                        ins.then_inc(s_fh, 1)
                if st is None or st + 1 < SLOTS:
                    transpose_tokens(s + 1, (r + 1) % WR, m + (r + 1) // WR, None if st is None else st + 1)
                if st is None or st >= 1:
                    v = (r - 1) % WR
                    pe.wait_ge(s_fte, s)
                    if st is None or st >= 2:
                        pe.wait_ge(s_fo, s - 1)
                    else:
                        pe.wait_ge(s_rd, 3)
                    for k in range(HB):
                        ins = mm(accp[:, 0:F], hidT[:, k, :], wexp[:, v, 2, k * F:(k + 1) * F], start=k == 0,
                                 stop=k == HB - 1)
                    ins.then_inc(s_fy, 1)
                if here:
                    pe.wait_ge(s_fm, s + 1)
                    if st is None or st >= 1:
                        pe.wait_ge(s_fte, s)
                    for k in range(HB):
                        ins = tr(tp2[:, k * P:(k + 1) * P], hid[:, k:HID:HB])
                    ins.then_inc(s_fth, 1)

            slot_iterations(pe, slot)


INS = ["x", "adj", "L0_gnn_W", "L0_gnn_a", "L0_gnn_w_ih", "L0_gnn_w_hh", "L0_gnn_b_ih", "L0_gnn_b_hh",
       "L0_ffn_gate_w", "L0_ffn_gate_b", "L0_ffn_w1", "L0_ffn_w2", "L0_ffn_w3"]


def kernel(**inputs):
    import numpy as np
    import concourse.bacc as bacc
    from concourse.bass_utils import run_bass_kernel_spmd

    nc = bacc.Bacc("TRN2", target_bir_lowering=False, num_devices=1)
    arrays, args = {}, []
    for name in INS:
        v = np.ascontiguousarray(inputs[name])
        arrays["in_" + name] = v
        args.append(nc.dram_tensor("in_" + name, v.shape, mybir.dt.from_np(v.dtype), kind="ExternalInput").ap())
    n, f = inputs["x"].shape
    out = nc.dram_tensor("out", (n, f), F32, kind="ExternalOutput").ap()
    rows = nc.dram_tensor("token_rows", (n, f + 4), F32, kind="Internal").ap()
    gnn_moe(nc, *args, out, rows)
    return run_bass_kernel_spmd(nc, [arrays], core_ids=[0]).results[0]["out"]
```

```python
from contextlib import ExitStack

import concourse.bass as bass
from concourse import mybir

F32 = mybir.dt.float32
F32R = mybir.dt.float32r
BF16 = mybir.dt.bfloat16
I32 = mybir.dt.int32
U32 = mybir.dt.uint32
ACT = mybir.ActivationFunctionType
ALU = mybir.AluOpType
AX = mybir.AxisListType

P = 128
EPS = 1e-5
SLOPE = 0.2
DS = 1.0 / 256.0


def gnn_moe(nc, x, adj, W, a, w_ih, w_hh, b_ih, b_hh, gate_w, gate_b, w1, w2, w3, out, rows):
    N, F = x.shape
    T = N // P
    KB = F // P
    NE, _, HID = w1.shape
    HB = HID // P
    G3 = 3 * F
    VW = F + 2
    HC = 1024
    Q = N // HC
    MC = 512
    CPT = N // MC
    JB = MC // P
    CQ = HC // MC
    RW = F + 4
    SLOTS = (2 * N + NE * (P - 1)) // P
    WR = 4
    WB = 4


    ctx = ExitStack()
    with ctx:
        def sem(name):
            return ctx.enter_context(nc.semaphore(name))

        def sb(name, shape, dt, stack=ctx):
            return stack.enter_context(nc.sbuf_tensor(name, shape, dt))

        bank = [ctx.enter_context(nc.psum_tensor(f"bank{i}", [P, 512], F32)) for i in range(6)]
        pT = [ctx.enter_context(nc.psum_tensor(f"pT{i}", [P, 2 * MC], BF16)) for i in range(2)]
        accp, accm, rzb, nb, tp, tp2 = bank

        ident = sb("ident", [P, P], F32)
        identb = sb("identb", [P, P], BF16)
        onesf = sb("onesf", [P, P], F32)
        before = sb("before", [P, P], BF16)
        onesb = sb("onesb", [P, P], BF16)
        iota_e = sb("iota_e", [P, NE], F32)
        pick = sb("pick", [P, 2, T, NE], BF16)
        gbias = sb("gbias", [P, NE], F32)
        gwt = sb("gwt", [P, KB, NE], F32)

        gs = ExitStack()
        V = sb("V", [P, T, 4, VW], F32R, gs)
        Dp = sb("Dp", [P, N], F32, gs)
        adjb = sb("adjb", [P, Q, HC], BF16, gs)
        gbuf = sb("gbuf", [P, HC], BF16, gs)
        tbuf = sb("tbuf", [P, 2, HC], BF16, gs)
        mask = sb("mask", [P, 2, 2, MC], F32R, gs)
        wT = sb("wT", [P, 2, KB, G3], F32, gs)
        xin = sb("xin", [P, 4, F], F32, gs)
        xnb = sb("xnb", [P, 2, F], F32, gs)
        hT = sb("hT", [P, 2 * KB, P], F32, gs)
        scr = sb("scr", [P, 6 * F], F32, gs)
        comb = sb("comb", [P, VW], F32, gs)
        xrow = sb("xrow", [P, 2, RW], F32, gs)
        xn2T = sb("xn2T", [P, KB, P], F32, gs)
        bias_rz = sb("bias_rz", [P, 2 * F], F32, gs)
        bias_n = sb("bias_n", [P, 2 * F], F32, gs)
        xmv = sb("xmv", [P, T, 2], F32, gs)
        rstd = sb("rstd", [P, T], F32, gs)
        sd = sb("sd", [P, T, 2], F32, gs)
        BD = sb("BD", [P, T, 2], F32, gs)
        bst = sb("bst", [P, 4, 6], F32, gs)
        mv4 = sb("mv4", [P, 4, 2], F32, gs)
        mv = sb("mv", [P, 2], F32, gs)
        dmx = sb("dmx", [P, 2, Q], F32, gs)
        co = sb("co", [P, 2, 6], F32, gs)
        rden = sb("rden", [P, 1], F32, gs)
        var = sb("var", [P, 1], F32, gs)
        rs = sb("rs", [P, 1], F32, gs)
        mhalf = sb("mhalf", [P, 1], F32, gs)
        lg = sb("lg", [P, NE], F32, gs)
        top = sb("top", [P, 8], F32, gs)
        tix = sb("tix", [P, 8], U32, gs)
        rt = sb("rt", [P, 3], F32, gs)
        rz = scr[:, 0:2 * F]
        nn = scr[:, 2 * F:4 * F]
        hp = scr[:, 4 * F:5 * F]
        dd = scr[:, 5 * F:6 * F]
        wnat = scr[:, :].rearrange("p (r f) -> p r f", f=F)
        diag = scr[:, 0:4 * P].rearrange("p (t m) -> p t m", m=P)
        WXW = F + 3
        Wx = xrow[:, :, 0:WXW]
        xs = adjb[:, :, :].rearrange("p q c -> p (q c)")[:, 0:16 * F].bitcast(F32)\
            .rearrange("p (b t f) -> p b t f", b=2, f=F)
        thr = sd[:, :, 1]
        dbc = pT[0][:, :].bitcast(F32)
        x1 = xin[:, 2, :]
        a_row = bias_rz[:, :]
        bhh_rz = xin[:, 2:4, :].rearrange("p a f -> p (a f)")
        gs.close()

        fs = ExitStack()
        wexp = sb("wexp", [P, WB, 3, KB * HID], F32, fs)
        xg = sb("xg", [P, WR, RW], F32, fs)
        xT = sb("xT", [P, WR, KB, P], F32, fs)
        sil = sb("sil", [P, HID], F32, fs)
        hid = sb("hid", [P, HID], F32, fs)
        hidT = sb("hidT", [P, HB, P], F32, fs)
        ysc = sb("ysc", [P, WR, F], F32, fs)
        lanew = sb("lanew", [P, WR, 2], F32, fs)
        iota_q = sb("iota_q", [P, P], F32, fs)
        cnt = sb("cnt", [P, NE, T], F32, fs)
        scan = sb("scan", [P, NE, T], F32, fs)
        ones = sb("ones", [P, NE, T], F32, fs)
        posw = sb("posw", [P, T, NE], F32, fs)
        prod = sb("prod", [P, 2, T, NE], F32, fs)
        pos = sb("pos", [P, 2, T], F32, fs)
        posi = sb("posi", [P, 2, T], I32, fs)
        poss = sb("poss", [P, 2, T], I32, fs)
        sidx = sb("sidx", [P, 2, T], F32, fs)
        qidx = sb("qidx", [P, 2, T], F32, fs)
        tok = sb("tok", [P, T], F32, fs)
        r16 = sb("r16", [P, 8, NE], F32, fs)
        kio = sb("kio", [P, T], F32, fs)
        cmp1 = sb("cmp1", [P, NE, T], F32, fs)
        sio = sb("sio", [P, SLOTS], F32, fs)
        cmp2 = sb("cmp2", [P, SLOTS, NE], F32, fs)
        esl = sb("esl", [P, SLOTS], F32, fs)
        esc = sb("esc", [P, SLOTS], F32, fs)
        fresh = sb("fresh", [P, SLOTS], F32, fs)
        order = sb("order", [P, SLOTS], F32, fs)
        ordi = sb("ordi", [P, SLOTS], I32, fs)
        slot_tab = sb("slot_tab", [P, 3, SLOTS], I32, fs)
        sv = sb("sv", [P, SLOTS], F32, fs)
        gidx = sb("gidx", [P, SLOTS], U32, fs)
        cidx = sb("cidx", [P, SLOTS], U32, fs)
        gi1 = sb("gi1", [P, WR, 1], U32, fs)
        ci1 = sb("ci1", [P, WR, 1], U32, fs)
        lane_hot = sb("lane_hot", [P, 8, P], F32, fs)
        slot_hot = sb("slot_hot", [P, 8, SLOTS], F32, fs)
        fs.close()

        s_const = sem("constants_made")
        s_cld = sem("small_inputs_loaded")
        s_bld = sem("biases_loaded")
        s_wn = sem("gru_weights_loaded")
        s_wtr = sem("gru_weights_transposed")
        s_wev = sem("gru_weights_copied")
        s_wx = sem("W_extended")
        s_x = [sem(f"x_loaded{r}") for r in range(4)]
        s_xs = [sem(f"x_group_loaded{u}") for u in range(2)]
        s_xsu = [sem(f"x_group_used{u}") for u in range(2)]
        s_var1 = sem("variance_of_x_done")
        s_rs1 = sem("deviation_of_x_done")
        s_var2 = sem("variance_of_x1_done")
        s_rs2 = sem("deviation_of_x1_done")
        s_xn = sem("xn_made")
        s_xt = sem("xn_transposed")
        s_xe = sem("xnT_copied")
        s_wh = sem("Wh_done")
        s_bd = sem("value_scales_done")
        s_hi = sem("value_hi_done")
        s_lo = sem("value_lo_done")
        s_dc = sem("d_diagonals_done")
        s_db = sem("d_broadcast")
        s_dpe = sem("d_broadcast_copied")
        s_vh = sem("denominator_hi_done")
        s_vd = sem("values_complete")
        s_link = sem("dve_link")
        s_adj = [sem(f"adj_loaded{q}") for q in range(Q)]
        s_t = sem("signed_adj_done")
        s_tr = sem("adj_transposed")
        s_mask = sem("masks_done")
        s_mm = sem("chunk_accumulated")
        s_nmx = sem("row_max_done")
        s_co = sem("row_scales_done")
        s_af = sem("accumulators_read")
        s_hp = sem("h_prime_done")
        s_xb = sem("xn_remade")
        s_th = sem("h_transposed")
        s_hT = sem("hT_copied")
        s_gru = sem("gru_products_done")
        s_rz = sem("rz_logits_done")
        s_gf = sem("gru_products_read")
        s_rzt = sem("rz_tanh_done")
        s_np = sem("n_logits_done")
        s_nt = sem("n_tanh_done")
        s_x1 = sem("x1_done")
        s_x1s = sem("x1_stored")
        s_xr = [sem(f"x_reloaded{u}") for u in range(2)]
        s_ln2 = sem("xn2_done")
        s_t2 = sem("xn2_transposed")
        s_t2e = sem("xn2T_copied")
        s_lgt = sem("gate_products_done")
        s_lg = sem("gate_logits_done")
        s_dl = sem("gate_difference_done")
        s_de = sem("gate_exp_done")
        s_row = sem("token_row_done")
        s_rows = [sem(f"token_row_stored{u}") for u in range(2)]
        s_rk = sem("ranks_done")
        s_io = sem("iotas_done")
        s_hot = sem("pair_one_hots_done")
        s_pl = sem("pair_placed")
        s_rd = sem("routing_done")
        s_tab = sem("slot_table_done")
        s_w = [sem(f"expert_weights_loaded{r}") for r in range(WR)]
        s_gc = sem("gather_index_copied")
        s_cc = sem("scatter_index_copied")
        s_g = [sem(f"tokens_gathered{r}") for r in range(WR)]
        s_sc = sem("outputs_added")
        s_lw = sem("lane_weights_done")
        s_ftx = sem("slot_tokens_transposed")
        s_fxe = sem("slot_tokensT_copied")
        s_fh = sem("up_products_done")
        s_fs = sem("silu_done")
        s_fm = sem("hidden_done")
        s_fth = sem("hidden_transposed")
        s_fte = sem("hiddenT_copied")
        s_fy = sem("expert_outputs_done")
        s_fo = sem("weighted_outputs_done")

        block = ctx.enter_context(nc.Block())

        def tile_iterations(eng, body):
            for r in range(4):
                body(r, r, 0, r)
            with eng.Fori(1, T // 4) as g:
                for r in range(4):
                    body(g * 4 + r, r, g, None)
            for r in range(4):
                body(T + r, r, T // 4, T + r)

        LAST = T + 3
        L0 = 4
        NL = (T - 1 - L0) // 2
        L1 = L0 + 2 * NL

        def graph_iterations(eng, body):
            for i in range(L0):
                body(i, i % 2, i // 2, i)
            with eng.Fori(0, NL) as m:
                for n in range(2):
                    body(m * 2 + (L0 + n), (L0 + n) % 2, m + (L0 + n) // 2, None)
            for i in range(L1, LAST):
                body(i, i % 2, i // 2, i)

        def live(static, lag):
            return static is None or 0 <= static - lag < T

        def after(static, lag, n):
            return static is None or static - lag >= n

        def pair_iterations(eng, body):
            for k in range(8):
                body(k // 2, k % 2, k, k // 2)
            with eng.Fori(1, T // 4 - 1) as m:
                for k in range(8):
                    body(m * 4 + k // 2, k % 2, k, None)
            for k in range(8):
                body(T - 4 + k // 2, k % 2, k, T - 4 + k // 2)

        FULL = (SLOTS - 2) // WR

        def slot_iterations(eng, body):
            for s in range(2 * WR):
                body(s, s % WR, s // WR, s)
            with eng.Fori(2, FULL) as m:
                for r in range(WR):
                    body(m * WR + r, r, m, None)
            for s in range(FULL * WR, SLOTS + 1):
                body(s, s % WR, s // WR, s)

        def at(t, size=1):
            return slice(t, t + size) if isinstance(t, int) else bass.ds(t, size)

        EXPERT, NEW, BUF = range(3)

        def table(eng, k, s):
            return eng.value_load(slot_tab[0:1, k, at(s)], min_val=0, max_val=(NE - 1, 1, WB - 1)[k])

        def one(b):
            return bass.ds(b, 1)

        def wh_bank(r):
            return (rzb, nb, accp, accm)[r % 4]

        def wait_apart(eng, *waits):
            held = [(semaphore, v if isinstance(v, int) else eng.to_reg(v)) for semaphore, v in waits]
            eng.wait_ge(s_const, CONSTS)
            for semaphore, v in held:
                eng.wait_ge(semaphore, v)

        CONSTS = 10
        @block.sync
        def _(sp):
            row = lambda b, lo, hi: b[lo:hi].rearrange("(o f) -> o f", o=1).broadcast_to([P, hi - lo])
            sp.dma_start(Wx[:, :, 0:F], W.rearrange("(k p) f -> p k f", p=P)).then_inc(s_cld, 16)
            sp.dma_start(a_row, a.rearrange("f o -> o f").broadcast_to([P, 2 * F])).then_inc(s_cld, 16)
            sp.dma_start(gwt[:, :, :], gate_w.rearrange("(k p) e -> p k e", p=P)).then_inc(s_cld, 16)
            sp.dma_start(gbias[:, :], row(gate_b, 0, NE)).then_inc(s_cld, 16)
            sp.dma_start(wnat, w_ih.rearrange("(r p) f -> p r f", p=P)).then_inc(s_wn, 16)
            groups = x.rearrange("(t p) f -> p t f", p=P)
            for u in range(2):
                sp.dma_start(xs[:, u, :, :], groups[:, 4 * u:4 * u + 4, :]).then_inc(s_xs[u], 16)
            for r in range(4):
                sp.dma_start(xin[:, r, :], x[r * P:(r + 1) * P, :]).then_inc(s_x[r], 16)
            with sp.Fori(1, T // 8) as g:
                for u in range(2):
                    sp.wait_ge(s_xsu[u], g)
                    sp.dma_start(xs[:, u, :, :], groups[:, bass.ds(g * 8 + 4 * u, 4), :]).then_inc(s_xs[u], 16)
            sp.wait_ge(s_wx, 3 * KB)
            sp.dma_start(bias_rz[:, :], row(b_ih, 0, 2 * F)).then_inc(s_bld, 16)
            sp.dma_start(bias_n[:, 0:F], row(b_ih, 2 * F, 3 * F)).then_inc(s_bld, 16)
            sp.dma_start(bias_n[:, F:2 * F], row(b_hh, 2 * F, 3 * F)).then_inc(s_bld, 16)
            with sp.Fori(1, T // 4) as g:
                for r in range(4):
                    sp.wait_ge(s_xn, g * 4 + (r - 3))
                    sp.dma_start(xin[:, r, :], x[bass.ds((g * 4 + r) * P, P), :]).then_inc(s_x[r], 16)
            sp.wait_ge(s_xn, T)
            sp.dma_start(bhh_rz, row(b_hh, 0, 2 * F)).then_inc(s_bld, 16)

            def body(i, u, h, st):
                if live(st, 1):
                    if after(st, 1, 2):
                        sp.wait_ge(s_x1, i - 2)
                    sp.dma_start(xin[:, (u + 1) % 2, :], x[at((i - 1) * P, P), :]).then_inc(s_xr[(u + 1) % 2], 16)
                if live(st, 2):
                    sp.wait_ge(s_x1, i - 1)
                    sp.dma_start(out[at((i - 2) * P, P), :], x1).then_inc(s_x1s, 16)
                if live(st, 3):
                    sp.wait_ge(s_row, i - 2)
                    sp.dma_start(rows[at((i - 3) * P, P), :], xrow[:, (u + 1) % 2, :]).then_inc(s_rows[(u + 1) % 2], 16)

            graph_iterations(sp, body)

            w1v, w2v = (w.rearrange("e (p k) h -> e p (k h)", k=KB) for w in (w1, w2))
            w3v = w3.rearrange("e (p k) o -> e p (k o)", k=HB)
            sp.wait_ge(s_tab, 3)

            def load(s, r, m, st):
                if st == SLOTS:
                    return
                e, new, b = (table(sp, k, s) for k in (EXPERT, NEW, BUF))
                if st is None or st >= WB:
                    wait_apart(sp, (s_fy, s - (WB - 1)))
                for n, wv in enumerate((w1v, w2v, w3v)):
                    sp.dma_start(wexp[:, one(b), n, :].rearrange("p o f -> p (o f)"),
                                 wv[one(e), :, :].rearrange("o p f -> (o p) f"), cond=new == 1).then_inc(s_w[r], 16)

            slot_iterations(sp, load)
            sp.wait_ge(s_sc, 16 * SLOTS)

        @block.gpsimd
        def _(pool):
            def load_adj(t, q):
                pool.dma_start(adjb[:, q, :], adj[at(t * P, P), q * HC:(q + 1) * HC]).then_inc(s_adj[q], 16)

            nc.gpsimd.memset(ident[:], 0.0).then_inc(s_const, 1)
            nc.gpsimd.memset(before[:], 1.0).then_inc(s_const, 1)
            nc.gpsimd.memset(onesb[:], 1.0).then_inc(s_const, 1)
            nc.gpsimd.memset(onesf[:], 1.0).then_inc(s_const, 1)
            nc.gpsimd.memset(mhalf[:], -0.5).then_inc(s_const, 1)
            nc.gpsimd.memset(V[:, :, :, F + 1:F + 2].bitcast(F32), 0.0).then_inc(s_const, 1)
            nc.gpsimd.iota(iota_e[:], [[1, NE]], base=0, channel_multiplier=0,
                           allow_small_or_imprecise_dtypes=True).then_inc(s_const, 1)
            pool.wait_ge(s_const, 7)
            nc.gpsimd.affine_select(out=ident[:], in_=ident[:], compare_op=ALU.not_equal, fill=1.0, base=0,
                                    pattern=[[-1, P]], channel_multiplier=1).then_inc(s_const, 1)
            nc.gpsimd.affine_select(out=before[:], in_=before[:], compare_op=ALU.is_gt, fill=0.0, base=0,
                                    pattern=[[1, P]], channel_multiplier=-1).then_inc(s_const, 1)
            pool.wait_ge(s_const, 9)
            nc.gpsimd.tensor_copy(identb[:], ident[:]).then_inc(s_const, 1)
            with pool.Fori(0, T // 4) as g:
                wait_apart(pool, (s_var1, g + 1))
                dev = rstd[:, at(g * 4, 4)]
                nc.gpsimd.tensor_tensor(dev, dev, mhalf[:, :].broadcast_to([P, 4]), ALU.pow).then_inc(s_rs1, 1)
            for q in range(Q):
                load_adj(0, q)

            def body(i, u, h, st):
                if st is None or st + 1 < T:
                    for q in range(Q):
                        pool.wait_ge(s_t, i * Q + (q + 1))
                        load_adj(i + 1, q)
                if live(st, 2):
                    pool.wait_ge(s_var2, i - 1)
                    nc.gpsimd.tensor_tensor(rs[:, :], var[:, :], mhalf[:, :], ALU.pow).then_inc(s_rs2, 1)

            graph_iterations(pool, body)

            pool.wait_ge(s_row, T)
            for par in range(2):
                pool.wait_ge(s_rows[par], 16 * (T // 2))
            pool.wait_ge(s_x1s, 16 * T)
            imp = dict(allow_small_or_imprecise_dtypes=True)
            nc.gpsimd.iota(sio[:], [[1, SLOTS]], base=0, channel_multiplier=0, **imp).then_inc(s_io, 1)
            nc.gpsimd.iota(kio[:], [[P, T]], base=0, channel_multiplier=0, **imp).then_inc(s_io, 1)
            nc.gpsimd.iota(iota_q[:], [[1, P]], base=0, channel_multiplier=0, **imp).then_inc(s_io, 1)
            nc.gpsimd.iota(tok[:], [[P, T]], base=1, channel_multiplier=1, **imp).then_inc(s_io, 1)
            nc.gpsimd.memset(ones[:], 1.0).then_inc(s_io, 1)

            def gather(s, r, m, st):
                if st is None or st >= WR:
                    pool.wait_ge(s_lw, s - (WR - 1))
                    pool.wait_ge(s_ftx, s - (WR - 1))
                nc.gpsimd.tensor_copy(gi1[:, r, :], gidx[:, at(s)]).then_inc(s_gc, 1)
                wait_apart(pool, (s_gc, s + 1))
                nc.gpsimd.indirect_dma_start(
                    out=xg[:, r, :], out_offset=None, in_=rows[:, :],
                    in_offset=bass.IndirectOffsetOnAxis(ap=gi1[:, r, :], axis=0)).then_inc(s_g[r], 16)

            def scatter(s, r, m, st):
                nc.gpsimd.tensor_copy(ci1[:, r, :], cidx[:, at(s)]).then_inc(s_cc, 1)
                waits = [(s_cc, s + 1), (s_fo, s + 1)]
                if st is None or st >= 1:
                    waits.append((s_sc, s * 16))
                wait_apart(pool, *waits)
                nc.gpsimd.indirect_dma_start(
                    out=out[:, :], out_offset=bass.IndirectOffsetOnAxis(ap=ci1[:, r, :], axis=0),
                    in_=ysc[:, r, :], in_offset=None, compute_op=ALU.add,
                    bounds_check=N - 1, oob_is_err=False).then_inc(s_sc, 16)

            pool.wait_ge(s_rd, 2)
            gather(0, 0, 0, 0)
            gather(1, 1, 0, 1)

            def slot(s, r, m, st):
                if st is None or st + 2 < SLOTS:
                    gather(s + 2, (r + 2) % WR, m + (r + 2) // WR, None if st is None else st + 2)
                if st is None or st >= 1:
                    scatter(s - 1, (r - 1) % WR, m + (r - 1) // WR, None if st is None else st - 1)

            slot_iterations(pool, slot)

        @block.scalar
        def _(act):
            act_copy = lambda o, i: nc.scalar.activation(o, i, ACT.Copy)

            def copy_gru_weights(m):
                for n in range(2 * KB):
                    kb, half = n // 2, n % 2
                    act.wait_ge(s_wtr, 2 * KB * m + n + 1)
                    act_copy(wT[:, m, kb, half * 3 * P:(half + 1) * 3 * P],
                             (accp, accm)[n % 2][:, 0:3 * P]).then_inc(s_wev, 1)

            copy_gru_weights(0)
            act.dma_start(wnat, w_hh.rearrange("(r p) f -> p r f", p=P)).then_inc(s_wn, 16)
            copy_gru_weights(1)

            def values(i, r, g, st):
                if live(st, 1):
                    act.wait_ge(s_wh, i)
                    nc.scalar.activation(BD[:, at(i - 1), :], wh_bank(r - 1)[:, F:F + 2], ACT.Exp).then_inc(s_bd, 1)
                if live(st, 0):
                    act.wait_ge(s_xt, i + 1)
                    if after(st, 0, 2):
                        act.wait_ge(s_wh, i - 1)
                    p = r % 2
                    act_copy(hT[:, KB * p:KB * p + KB, :].rearrange("p k m -> p (k m)"),
                             (tp, tp2)[p][:, 0:F]).then_inc(s_xe, 1)
                if live(st, 1):
                    act.wait_ge(s_bd, i)
                    for k in range(2):
                        nc.scalar.activation(V[:, at(i - 1), 2 * k, 0:F], wh_bank(r - 1)[:, 0:F], ACT.Copy,
                                             scale=BD[:, at(i - 1), k]).then_inc(s_hi, 1)
                if r == 3 and (st is None or st > 3):
                    act.wait_ge(s_db, g)
                    act_copy(Dp[:, at((g - 1) * 4 * P, 4 * P)], dbc).then_inc(s_dpe, 1)

            tile_iterations(act, values)
            for k in range(2):
                act_copy(V[:, :, 2 * k, F], BD[:, :, k]).then_inc(s_vh, 1)

            def masks(i, c, st):
                C = i * CPT + c
                act.wait_ge(s_tr, C + 1)
                if st is None or st * CPT + c >= 2:
                    act.wait_ge(s_mm, C - 1)
                for k, sign in enumerate((2.0, -2.0)):
                    ins = nc.scalar.activation(mask[:, c % 2, k, :], pT[c % 2][:, 0:MC], ACT.Relu, scale=sign)
                ins.then_inc(s_mask, 1)

            masks(0, 0, 0)

            def rz_tanh(i, u):
                act.wait_ge(s_rz, i - 1)
                nc.scalar.activation(rz, rz, ACT.Tanh, scale=0.5).then_inc(s_rzt, 1)

            def n_tanh(i, u):
                act.wait_ge(s_np, i - 1)
                nc.scalar.activation(nn[:, 0:F], nn[:, 0:F], ACT.Tanh).then_inc(s_nt, 1)

            def copy_hT(i, u, st):
                act.wait_ge(s_th, i)
                if after(st, 1, 1):
                    act.wait_ge(s_gru, i - 1)
                act_copy(hT[:, :, :].rearrange("p k m -> p (k m)"), tp[:, :]).then_inc(s_hT, 1)

            def gate_exp(i, u):
                act.wait_ge(s_dl, i - 2)
                nc.scalar.activation(rt[:, 1:2], rt[:, 0:1], ACT.Exp).then_inc(s_de, 1)

            def row_scales(i, u):
                act.wait_ge(s_nmx, i + 1)
                for k, slope in enumerate((1.0, SLOPE)):
                    ins = nc.scalar.activation(co[:, u, k:k + 1], thr[:, at(i)], ACT.Exp, scale=-slope / DS,
                                               bias=co[:, u, 5:6])
                ins.then_inc(s_co, 1)

            def body(i, u, h, st):
                for c in range(CPT):
                    if c and live(st, 0):
                        masks(i, c, st)
                    if c == 0 and live(st, 3):
                        act.wait_ge(s_t2, i - 2)
                        act_copy(xn2T[:, :, :].rearrange("p k m -> p (k m)"), tp2[:, 0:F]).then_inc(s_t2e, 1)
                    if c == 1 and live(st, 2):
                        rz_tanh(i, u)
                    if c == min(3, CPT - 1) and live(st, 1):
                        copy_hT(i, u, st)
                    if c == min(4, CPT - 1):
                        if live(st, 2):
                            n_tanh(i, u)
                        if live(st, 3):
                            gate_exp(i, u)
                    if c == min(6, CPT - 1) and live(st, 0):
                        row_scales(i, u)
                if st is None or st + 1 < T:
                    masks(i + 1, 0, None if st is None else st + 1)

            graph_iterations(act, body)

            def copy_slot_xT(s, r, st):
                act.wait_ge(s_ftx, s + 1)
                if st is None or st >= WR:
                    act.wait_ge(s_fh, (s - (WR - 1)) * 2)
                act_copy(xT[:, r, :, :].rearrange("p k m -> p (k m)"), tp[:, 0:F]).then_inc(s_fxe, 1)

            copy_slot_xT(0, 0, 0)

            def slot(s, r, m, st):
                if st == SLOTS:
                    return
                act.wait_ge(s_fh, s * 2 + 1)
                if st is None or st >= 1:
                    act.wait_ge(s_fm, s)
                nc.scalar.activation(sil[:, :], rzb[:, :], ACT.Silu).then_inc(s_fs, 1)
                if st is None or st + 1 < SLOTS:
                    copy_slot_xT(s + 1, (r + 1) % WR, None if st is None else st + 1)
                act.wait_ge(s_fth, s + 1)
                if st is None or st >= 1:
                    act.wait_ge(s_fy, s)
                act_copy(hidT[:, :, :].rearrange("p k m -> p (k m)"), tp2[:, :]).then_inc(s_fte, 1)

            slot_iterations(act, slot)

        @block.vector
        def _(dve):
            V_ = nc.vector
            done = [0]

            def link(ins, alone=False):
                done[0] = done[0] + 1
                ins.then_inc(s_link, 1)
                if alone:
                    wait_apart(dve, (s_link, done[0]))
                else:
                    dve.wait_ge(s_link, done[0])

            dve.wait_ge(s_cld, 64)
            for kb in range(KB):
                for n, (half, scale) in enumerate(((1, 1.0), (1, SLOPE), (0, -1.0))):
                    V_.tensor_tensor_reduce(out=comb[:, 0:F], in0=Wx[:, kb, 0:F], in1=a_row[:, half * F:half * F + F],
                                            scale=scale, scalar=0.0, op0=ALU.mult, op1=ALU.add,
                                            accum_out=Wx[:, kb, F + n:F + n + 1]).then_inc(s_wx, 1)
                    dve.wait_ge(s_wx, 3 * kb + n + 1)

            MOMENT_LINKS = 2
            with dve.Fori(0, T // 8) as g:
                for u in range(2):
                    done[0] = (g * 2 + u) * MOMENT_LINKS
                    dve.wait_ge(s_xs[u], g * 16 + 16)
                    for r in range(3):
                        V_.bn_stats(bst[:, r, :], xs[:, u, r, :])
                    ins = V_.bn_stats(bst[:, 3, :], xs[:, u, 3, :])
                    ins.then_inc(s_xsu[u], 1)
                    wait_apart(dve, (s_xsu[u], g + 1))
                    for r in range(3):
                        V_.bn_aggr(mv4[:, r, :], bst[:, r, :])
                    link(V_.bn_aggr(mv4[:, 3, :], bst[:, 3, :]))
                    V_.tensor_scalar(rstd[:, at(g * 8 + 4 * u, 4)], mv4[:, :, 1], EPS, None, ALU.add).then_inc(s_var1, 1)
                    link(V_.tensor_copy(xmv[:, at(g * 8 + 4 * u, 4), :], mv4[:, :, :]))
            done[0] = T // 4 * MOMENT_LINKS

            def moments(src, var_done):
                link(V_.bn_stats(bst[:, 0, :], src), True)
                link(V_.bn_aggr(mv[:, :], bst[:, 0, :]))
                V_.tensor_scalar(var[:, :], mv[:, 1:2], EPS, None, ALU.add).then_inc(var_done, 1)

            dve.wait_ge(s_rs1, T // 4)
            moment_links = done[0]

            def values(i, r, g, st):
                if live(st, 0):
                    dve.wait_ge(s_x[r], g * 16 + 16)
                    if after(st, 0, 2):
                        dve.wait_ge(s_xt, i - 1)
                    V_.tensor_scalar(xnb[:, r % 2, :], xin[:, r, :], xmv[:, at(i), 0:1], rstd[:, at(i)], ALU.subtract,
                                     ALU.mult).then_inc(s_xn, 1)
                if live(st, 2):
                    wh = wh_bank(r - 2)
                    dve.wait_ge(s_hi, (i - 1) * 2)
                    columns = V_.tensor_scalar(sd[:, at(i - 2), :], wh[:, F:F + 3:2], DS, None, ALU.mult)
                    if r == 1:
                        done[0] = moment_links + g - 1
                        link(columns)
                    for k in range(2):
                        V_.scalar_tensor_tensor(out=V[:, at(i - 2), 2 * k + 1, 0:F], in0=wh[:, 0:F],
                                                scalar=BD[:, at(i - 2), k], in1=V[:, at(i - 2), 2 * k, 0:F].bitcast(F32),
                                                op0=ALU.mult, op1=ALU.subtract).then_inc(s_lo, 1)
                if r == 1 and (st is None or st > 1):
                    V_.tensor_tensor(diag[:, :, :], ident[:, :].unsqueeze(1).broadcast_to([P, 4, P]),
                                     sd[:, at((g - 1) * 4, 4), 0:1].broadcast_to([P, 4, P]), ALU.mult).then_inc(s_dc, 1)

            tile_iterations(dve, values)
            done[0] = moment_links + T // 4
            for k in range(2):
                dve.wait_ge(s_vh, k + 1)
                V_.tensor_tensor(V[:, :, 2 * k + 1, F], BD[:, :, k], V[:, :, 2 * k, F].bitcast(F32),
                                 ALU.subtract).then_inc(s_vd, 1)
            dve.wait_ge(s_bld, 64)
            link(V_.tensor_tensor(bias_rz[:, :], bias_rz[:, :], bhh_rz, ALU.add))
            dve.wait_ge(s_dpe, T // 4)

            def piece(i, q, u, st):
                waits = [(s_adj[q], i * 16 + 16)]
                if st is None or st or q:
                    waits.append((s_t, i * Q + q))
                wait_apart(dve, *waits)
                cols = slice(q * HC, (q + 1) * HC)
                link(V_.tensor_tensor_reduce(out=gbuf[:, :], in0=Dp[:, cols], in1=adjb[:, q, :], scale=1.0, scalar=-1e30,
                                             op0=ALU.add, op1=ALU.max, accum_out=dmx[:, u, q:q + 1]))
                link(V_.tensor_scalar(gbuf[:, :], Dp[:, cols], thr[:, at(i)], 0.5, ALU.is_gt, ALU.subtract))
                if st is None or st * Q + q >= 2:
                    dve.wait_ge(s_tr, (i * Q + (q - 1)) * CQ)
                V_.tensor_tensor(tbuf[:, q % 2, :], adjb[:, q, :], gbuf[:, :], ALU.mult).then_inc(s_t, 1)

            def row_max(i, u):
                c = lambda k: co[:, u, k:k + 1]
                link(V_.tensor_reduce(c(2), dmx[:, u, :], AX.X, ALU.max))
                link(V_.tensor_scalar(c(3), c(2), 1.0, thr[:, at(i)], ALU.subtract, ALU.subtract))
                link(V_.tensor_scalar(c(4), c(3), -SLOPE / DS, None, ALU.mult))
                V_.scalar_tensor_tensor(out=c(5), in0=c(3), scalar=-1.0 / DS, in1=c(4), op0=ALU.mult,
                                        op1=ALU.min).then_inc(s_nmx, 1)

            def combine(i, u, st):
                v = (u + 1) % 2
                dve.wait_ge(s_mm, i * CPT)
                dve.wait_ge(s_co, i)
                link(V_.tensor_scalar(comb[:, 0:F + 1], accm[:, 0:F + 1], co[:, v, 1:2], None, ALU.mult))
                V_.scalar_tensor_tensor(out=comb[:, 0:F + 1], in0=accp[:, 0:F + 1], scalar=co[:, v, 0:1],
                                        in1=comb[:, 0:F + 1], op0=ALU.mult, op1=ALU.add).then_inc(s_af, 1)
                dve.wait_ge(s_af, i)
                link(V_.reciprocal(rden[:, :], comb[:, F:F + 1]))
                if after(st, 1, 1):
                    dve.wait_ge(s_th, i - 1)
                V_.tensor_scalar(hp, comb[:, 0:F], rden[:, 0:1], None, ALU.mult).then_inc(s_hp, 1)

            def remake_xn(i, u, h, st):
                v = (u + 1) % 2
                dve.wait_ge(s_xr[v], (h + (u - 1) // 2) * 16 + 16)
                V_.tensor_scalar(xnb[:, v, :], xin[:, v, :], xmv[:, at(i - 1), 0:1], rstd[:, at(i - 1)], ALU.subtract,
                                 ALU.mult).then_inc(s_xb, 1)

            def gru_logits(i):
                dve.wait_ge(s_gru, i - 1)
                V_.tensor_tensor(rz, rzb[:, :], bias_rz[:, :], ALU.add).then_inc(s_rz, 1)
                V_.tensor_tensor(nn, nb[:, :], bias_n[:, :], ALU.add).then_inc(s_gf, 1)

            def gru_n(i):
                dve.wait_ge(s_rzt, i - 1)
                dve.wait_ge(s_gf, i - 1)
                link(V_.scalar_tensor_tensor(out=nn[:, F:2 * F], in0=rz[:, 0:F], scalar=1.0, in1=nn[:, F:2 * F],
                                             op0=ALU.add, op1=ALU.mult))
                V_.scalar_tensor_tensor(out=nn[:, 0:F], in0=nn[:, F:2 * F], scalar=0.5, in1=nn[:, 0:F], op0=ALU.mult,
                                        op1=ALU.add).then_inc(s_np, 1)

            def gru_out(i, u, st):
                dve.wait_ge(s_nt, i - 1)
                link(V_.tensor_tensor(dd, xnb[:, u, :], nn[:, 0:F], ALU.subtract))
                link(V_.scalar_tensor_tensor(out=dd, in0=rz[:, F:2 * F], scalar=1.0, in1=dd, op0=ALU.add, op1=ALU.mult))
                link(V_.scalar_tensor_tensor(out=dd, in0=dd, scalar=0.5, in1=nn[:, 0:F], op0=ALU.mult, op1=ALU.add))
                if after(st, 2, 1):
                    dve.wait_ge(s_x1s, (i - 2) * 16)
                V_.tensor_tensor(x1, dd, xin[:, u, :], ALU.add).then_inc(s_x1, 1)

            def norm2(i, u, h, st):
                dve.wait_ge(s_x1, i - 1)
                moments(x1, s_var2)
                dve.wait_ge(s_rs2, i - 1)
                if after(st, 2, 2):
                    dve.wait_ge(s_rows[u], (h + (u - 4) // 2) * 16 + 16)
                V_.tensor_scalar(xrow[:, u, 0:F], x1, mv[:, 0:1], rs[:, 0:1], ALU.subtract, ALU.mult).then_inc(s_ln2, 1)

            def route_top(i, u):
                v = (u + 1) % 2
                dve.wait_ge(s_lgt, i - 2)
                V_.tensor_tensor(lg[:, :], tp2[:, F:F + NE], gbias[:, :], ALU.add).then_inc(s_lg, 1)
                wait_apart(dve, (s_lg, i - 2))
                link(V_.max(top[:, :], lg[:, :]))
                V_.tensor_tensor(rt[:, 0:1], top[:, 1:2], top[:, 0:1], ALU.subtract).then_inc(s_dl, 1)
                link(V_.max_index(tix[:, :], top[:, :], lg[:, :]))
                link(V_.tensor_copy(xrow[:, v, F + 2:F + 4], tix[:, 0:2]))
                for k in range(2):
                    V_.tensor_scalar(pick[:, k, at(i - 3), :], iota_e[:, :], xrow[:, v, F + 2 + k:F + 3 + k], None,
                                     ALU.is_equal)

            def route_weights(i, u):
                v = (u + 1) % 2
                dve.wait_ge(s_de, i - 2)
                link(V_.tensor_scalar(rt[:, 2:3], rt[:, 1:2], 1.0, None, ALU.add))
                link(V_.reciprocal(xrow[:, v, F:F + 1], rt[:, 2:3]))
                V_.tensor_tensor(xrow[:, v, F + 1:F + 2], rt[:, 1:2], xrow[:, v, F:F + 1], ALU.mult).then_inc(s_row, 1)

            piece(0, 0, 0, 0)
            loop_links = [None, None]
            ITER_LINKS = 2 * Q + 3 + 2 + 1 + 3 + 2 + 3 + 2

            def body(i, u, h, st):
                if st is None:
                    if loop_links[0] is None:
                        loop_links[0] = done[0]
                    done[0] = loop_links[0] + (i - L0) * ITER_LINKS
                elif loop_links[0] is not None and st == L1:
                    done[0] = loop_links[0] + (L1 - L0) * ITER_LINKS
                start = done[0]
                if live(st, 1):
                    combine(i, u, st)
                    remake_xn(i, u, h, st)
                if live(st, 0) and Q > 1:
                    piece(i, 1, u, st)
                if live(st, 2):
                    gru_logits(i)
                if live(st, 0) and Q > 2:
                    piece(i, 2, u, st)
                if live(st, 2):
                    gru_n(i)
                if live(st, 3):
                    route_top(i, u)
                if live(st, 0):
                    for q in range(3, Q):
                        piece(i, q, u, st)
                if live(st, 2):
                    gru_out(i, u, st)
                if live(st, 0):
                    row_max(i, u)
                if live(st, 3):
                    route_weights(i, u)
                if st is None or st + 1 < T:
                    piece(i + 1, 0, (u + 1) % 2, None if st is None else st + 1)
                if live(st, 2):
                    norm2(i, u, h, st)
                if st is not None and L0 <= st < T - 1:
                    assert done[0] - start == ITER_LINKS, (done[0] - start, ITER_LINKS)

            graph_iterations(dve, body)

            dve.wait_ge(s_rows[0], 16 * (T // 2))
            dve.wait_ge(s_rows[1], 16 * (T // 2))
            dve.wait_ge(s_x1s, 16 * T)
            dve.wait_ge(s_rk, 2)
            dve.wait_ge(s_io, 5)
            R = lambda k: r16[:, k, :]
            per_t = lambda v: v.unsqueeze(2).broadcast_to([P, NE, T])
            total, tiles, tend, tstart, tincl, estart, base = (R(k) for k in range(7))
            link(V_.tensor_copy(cnt[:, :, :], nb[:, 0:T * NE].rearrange("p (t e) -> p e t", e=NE)))
            link(V_.tensor_reduce(total, cnt[:, :, :], AX.X, ALU.add))
            flat = lambda v: v.rearrange("p e t -> p (e t)")
            link(V_.tensor_tensor_scan(flat(scan[:, :, :]), flat(ones[:, :, :]), flat(cnt[:, :, :]), 0.0, ALU.mult, ALU.add))
            link(V_.tensor_tensor(cmp1[:, :, :], per_t(total), kio[:, :].unsqueeze(1).broadcast_to([P, NE, T]), ALU.is_gt))
            link(V_.tensor_reduce(tiles, cmp1[:, :, :], AX.X, ALU.add))
            link(V_.tensor_tensor_scan(tend, ones[:, 0, 0:NE], tiles, 0.0, ALU.mult, ALU.add))
            link(V_.tensor_tensor_scan(tincl, ones[:, 0, 0:NE], total, 0.0, ALU.mult, ALU.add))
            link(V_.tensor_tensor(tstart, tend, tiles, ALU.subtract))
            link(V_.tensor_tensor(estart, tincl, total, ALU.subtract))
            link(V_.scalar_tensor_tensor(out=base, in0=tstart, scalar=float(P), in1=estart, op0=ALU.mult, op1=ALU.subtract))
            link(V_.tensor_tensor(cmp1[:, :, :], scan[:, :, :], cnt[:, :, :], ALU.subtract))
            link(V_.tensor_tensor(cmp1[:, :, :], cmp1[:, :, :], per_t(base), ALU.add))
            link(V_.tensor_tensor(posw[:, :, :].rearrange("p t e -> p e t"), cmp1[:, :, :],
                                  rzb[:, 0:T * NE].rearrange("p (t e) -> p e t", e=NE), ALU.add))
            for k in range(2):
                link(V_.tensor_tensor(prod[:, k, :, :], pick[:, k, :, :], posw[:, :, :], ALU.mult))
            link(V_.tensor_reduce(pos[:, :, :].rearrange("p k t -> p (k t)"),
                                  prod[:, :, :, :].rearrange("p k t e -> p (k t) e"), AX.X, ALU.add))
            link(V_.tensor_copy(posi[:, :, :], pos[:, :, :]))
            link(V_.tensor_single_scalar(poss[:, :, :], posi[:, :, :], P.bit_length() - 1, ALU.arith_shift_right))
            link(V_.tensor_copy(sidx[:, :, :], poss[:, :, :]))
            link(V_.scalar_tensor_tensor(out=qidx[:, :, :], in0=sidx[:, :, :], scalar=-float(P), in1=pos[:, :, :],
                                         op0=ALU.mult, op1=ALU.add))

            link(V_.tensor_tensor(cmp2[:, :, :], sio[:, :].unsqueeze(2).broadcast_to([P, SLOTS, NE]),
                                  tend.unsqueeze(1).broadcast_to([P, SLOTS, NE]), ALU.is_ge))
            link(V_.tensor_reduce(esc[:, :], cmp2[:, :, :], AX.X, ALU.add))
            link(V_.tensor_scalar(esl[:, :], esc[:, :], float(NE - 1), None, ALU.min))
            V_.tensor_copy(slot_tab[:, EXPERT, :], esl[:, :]).then_inc(s_tab, 1)
            link(V_.tensor_copy(fresh[:, 0:1], ones[:, 0, 0:1]))
            link(V_.tensor_tensor(fresh[:, 1:SLOTS], esl[:, 1:SLOTS], esl[:, 0:SLOTS - 1], ALU.not_equal))
            V_.tensor_copy(slot_tab[:, NEW, :], fresh[:, :]).then_inc(s_tab, 1)
            link(V_.tensor_tensor_scan(order[:, :], flat(ones[:, :, :])[:, 0:SLOTS], fresh[:, :], 0.0, ALU.mult, ALU.add))
            link(V_.tensor_copy(ordi[:, :], order[:, :]))
            V_.tensor_single_scalar(slot_tab[:, BUF, :], ordi[:, :], WB - 1, ALU.bitwise_and).then_inc(s_tab, 1)

            def pair(t, k, b, st):
                n = t * 2 + k
                if st is None or 2 * st + k >= 8:
                    dve.wait_ge(s_pl, n - 7)
                V_.tensor_scalar(lane_hot[:, b, :], iota_q[:, :], qidx[:, k, at(t)], None, ALU.is_equal)
                V_.tensor_scalar(slot_hot[:, b, :], sio[:, :], sidx[:, k, at(t)], tok[:, at(t)], ALU.is_equal,
                                 ALU.mult).then_inc(s_hot, 1)

            pair_iterations(dve, pair)
            dve.wait_ge(s_pl, 2 * T)
            V_.tensor_scalar(gidx[:, :], accp[:, 0:SLOTS], -1.0, 0.0, ALU.add, ALU.max).then_inc(s_rd, 1)
            link(V_.tensor_scalar(sv[:, :], accp[:, 0:SLOTS], 0.0, float(2 * N), ALU.is_equal, ALU.mult))
            V_.scalar_tensor_tensor(out=cidx[:, :], in0=accp[:, 0:SLOTS], scalar=-1.0, in1=sv[:, :], op0=ALU.add,
                                    op1=ALU.add).then_inc(s_rd, 1)

            slot_base = done[0]
            SLOT_LINKS = 2

            def slot(s, r, m, st):
                done[0] = slot_base + s * SLOT_LINKS
                if st is None or st < SLOTS:
                    dve.wait_ge(s_g[r], m * 16 + 16)
                    if st is None or st >= WR:
                        dve.wait_ge(s_fo, s - (WR - 1))
                    e = esl[:, at(s)]
                    link(V_.tensor_scalar(lanew[:, r, 0:1], xg[:, r, F + 2:F + 3], e, xg[:, r, F:F + 1],
                                          ALU.is_equal, ALU.mult))
                    link(V_.tensor_scalar(lanew[:, r, 1:2], xg[:, r, F + 3:F + 4], e, xg[:, r, F + 1:F + 2],
                                          ALU.is_equal, ALU.mult))
                    V_.tensor_tensor(lanew[:, r, 0:1], lanew[:, r, 0:1], lanew[:, r, 1:2], ALU.add).then_inc(s_lw, 1)
                    dve.wait_ge(s_fs, s + 1)
                    dve.wait_ge(s_fh, s * 2 + 2)
                    if st is None or st >= 1:
                        dve.wait_ge(s_fth, s)
                    V_.tensor_tensor(hid[:, :], nb[:, :], sil[:, :], ALU.mult).then_inc(s_fm, 1)
                if st is None or st >= 1:
                    v = (r - 1) % WR
                    dve.wait_ge(s_fy, s)
                    dve.wait_ge(s_lw, s)
                    if st is None or st >= WR + 1:
                        dve.wait_ge(s_sc, (s - WR) * 16)
                    V_.tensor_scalar(ysc[:, v, :], accp[:, 0:F], lanew[:, v, 0:1], None, ALU.mult).then_inc(s_fo, 1)

            slot_iterations(dve, slot)

        @block.tensor
        def _(pe):
            mm = nc.tensor.matmul
            tr = lambda o, i: nc.tensor.transpose(o, i, ident[:, :])

            def transpose_gru_weights(m):
                pe.wait_ge(s_wn, 16 * (m + 1))
                for n in range(2 * KB):
                    kb, half = n // 2, n % 2
                    if m or n >= 2:
                        pe.wait_ge(s_wev, 2 * KB * m + n - 1)
                    for r in range(3):
                        ins = tr((accp, accm)[n % 2][:, r * P:(r + 1) * P],
                                 wnat[:, half * 3 + r, kb * P:(kb + 1) * P])
                    ins.then_inc(s_wtr, 1)

            pe.wait_ge(s_const, CONSTS)
            transpose_gru_weights(0)
            transpose_gru_weights(1)
            pe.wait_ge(s_wx, 3 * KB)
            pe.wait_ge(s_wev, 4 * KB)

            def values(i, r, g, st):
                if live(st, 1):
                    pe.wait_ge(s_xe, i)
                    if after(st, 1, 4):
                        pe.wait_ge(s_lo, (i - 4) * 2)
                    for kb in range(KB):
                        ins = mm(wh_bank(r - 1)[:, 0:WXW], hT[:, KB * ((r - 1) % 2) + kb, :], Wx[:, kb, :],
                                 start=kb == 0, stop=kb == KB - 1)
                    ins.then_inc(s_wh, 1)
                if live(st, 0):
                    pe.wait_ge(s_xn, i + 1)
                    if after(st, 0, 2):
                        pe.wait_ge(s_xe, i - 1)
                    p = r % 2
                    for kb in range(KB):
                        ins = tr((tp, tp2)[p][:, kb * P:(kb + 1) * P], xnb[:, p, kb * P:(kb + 1) * P])
                    ins.then_inc(s_xt, 1)
                if r == 2 and (st is None or st > 2):
                    pe.wait_ge(s_dc, g)
                    mm(dbc, onesf[:, :], scr[:, 0:4 * P], start=True, stop=True).then_inc(s_db, 1)

            tile_iterations(pe, values)
            pe.wait_ge(s_dpe, T // 4)

            def transpose_adj(i, c, st):
                C = i * CPT + c
                q = c // CQ
                pe.wait_ge(s_t, i * Q + (q + 1))
                if st is None or st * CPT + c >= 2:
                    pe.wait_ge(s_mask, C - 1)
                for b in range(JB):
                    at0 = (c % CQ) * MC + b * P
                    ins = nc.tensor.transpose(pT[c % 2][:, b * P:(b + 1) * P], tbuf[:, q % 2, at0:at0 + P],
                                              identb[:, :])
                ins.then_inc(s_tr, 1)

            def accumulate(i, c, st):
                pe.wait_ge(s_mask, i * CPT + (c + 1))
                if c == 0 and after(st, 0, 1):
                    pe.wait_ge(s_af, i)
                for b in range(JB):
                    j = c * JB + b
                    for k, acc in enumerate((accp, accm)):
                        for part in range(2):
                            ins = mm(acc[:, 0:VW], mask[:, c % 2, k, b * P:(b + 1) * P], V[:, j, 2 * k + part, :],
                                     start=j == 0 and part == 0, stop=j == T - 1 and part == 1)
                ins.then_inc(s_mm, 1)

            def transpose_h(i, u, st):
                v = (u + 1) % 2
                pe.wait_ge(s_hp, i)
                pe.wait_ge(s_xb, i)
                if after(st, 1, 1):
                    pe.wait_ge(s_hT, i - 1)
                for n, src in enumerate((hp, xnb[:, v, :])):
                    for kb in range(KB):
                        ins = tr(tp[:, (n * KB + kb) * P:(n * KB + kb + 1) * P], src[:, kb * P:(kb + 1) * P])
                ins.then_inc(s_th, 1)

            def gru(i, st):
                pe.wait_ge(s_hT, i - 1)
                if after(st, 2, 1):
                    pe.wait_ge(s_gf, i - 2)
                for n in range(2 * KB):
                    mm(rzb[:, :], hT[:, n, :], wT[:, n // KB, n % KB, 0:2 * F], start=n == 0, stop=n == 2 * KB - 1)
                for n in range(2 * KB):
                    m, kb = n // KB, n % KB
                    ins = mm(nb[:, m * F:(m + 1) * F], hT[:, n, :], wT[:, m, kb, 2 * F:3 * F], start=kb == 0,
                             stop=kb == KB - 1)
                ins.then_inc(s_gru, 1)

            def transpose_x2(i, u, st):
                v = (u + 1) % 2
                pe.wait_ge(s_ln2, i - 2)
                if after(st, 3, 1):
                    pe.wait_ge(s_lg, i - 3)
                for kb in range(KB):
                    ins = tr(tp2[:, kb * P:(kb + 1) * P], xrow[:, v, kb * P:(kb + 1) * P])
                ins.then_inc(s_t2, 1)

            def gate(i):
                pe.wait_ge(s_t2e, i - 2)
                for kb in range(KB):
                    ins = mm(tp2[:, F:F + NE], xn2T[:, kb, :], gwt[:, kb, :], start=kb == 0, stop=kb == KB - 1)
                ins.then_inc(s_lgt, 1)

            pe.wait_ge(s_vd, 2)
            pe.wait_ge(s_lo, 2 * T)
            transpose_adj(0, 0, 0)

            def body(i, u, h, st):
                if live(st, 2):
                    gru(i, st)
                if live(st, 3):
                    transpose_x2(i, u, st)
                if live(st, 3) and not live(st, 0):
                    gate(i)
                for c in range(CPT):
                    if live(st, 0):
                        if c + 1 < CPT:
                            transpose_adj(i, c + 1, st)
                        elif st is None or st + 1 < T:
                            transpose_adj(i + 1, 0, None if st is None else st + 1)
                        accumulate(i, c, st)
                    if c == 0 and live(st, 3) and live(st, 0):
                        gate(i)
                    if c == min(2, CPT - 1) and live(st, 1):
                        transpose_h(i, u, st)

            graph_iterations(pe, body)

            pe.wait_ge(s_row, T)
            for lhs, acc in ((before, rzb), (onesb, nb)):
                for k in range(2):
                    ins = mm(acc[:, 0:T * NE], lhs[:, :], pick[:, k, :, :].rearrange("p t e -> p (t e)"), start=k == 0,
                             stop=k == 1)
                ins.then_inc(s_rk, 1)

            def place(t, k, b, st):
                pe.wait_ge(s_hot, t * 2 + (k + 1))
                mm(accp[:, 0:SLOTS], lane_hot[:, b, :], slot_hot[:, b, :], start=st == 0 and k == 0,
                   stop=st == T - 1 and k == 1).then_inc(s_pl, 1)

            pair_iterations(pe, place)

            def transpose_tokens(s, r, m, st):
                pe.wait_ge(s_g[r], m * 16 + 16)
                if st is None or st >= 1:
                    pe.wait_ge(s_fxe, s)
                for k in range(KB):
                    ins = tr(tp[:, k * P:(k + 1) * P], xg[:, r, k:F:KB])
                ins.then_inc(s_ftx, 1)

            pe.wait_ge(s_tab, 3)
            transpose_tokens(0, 0, 0, 0)

            def slot(s, r, m, st):
                here = st is None or st < SLOTS
                if here:
                    b = table(pe, BUF, s)
                    pe.wait_ge(s_w[r], m * 48 + 48)
                    pe.wait_ge(s_fxe, s + 1)
                    for n, acc in enumerate((rzb, nb)):
                        if st is None or st >= 1:
                            pe.wait_ge((s_fs, s_fm)[n], s)
                        for k in range(KB):
                            ins = mm(acc[:, 0:HID], xT[:, r, k, :],
                                     wexp[:, one(b), n, k * HID:(k + 1) * HID].rearrange("p o f -> p (o f)"),
                                     start=k == 0, stop=k == KB - 1)
                        ins.then_inc(s_fh, 1)
                if st is None or st + 1 < SLOTS:
                    transpose_tokens(s + 1, (r + 1) % WR, m + (r + 1) // WR, None if st is None else st + 1)
                if st is None or st >= 1:
                    b1 = table(pe, BUF, s - 1)
                    pe.wait_ge(s_fte, s)
                    if st is None or st >= 2:
                        pe.wait_ge(s_fo, s - 1)
                    else:
                        pe.wait_ge(s_rd, 2)
                    for k in range(HB):
                        ins = mm(accp[:, 0:F], hidT[:, k, :],
                                 wexp[:, one(b1), 2, k * F:(k + 1) * F].rearrange("p o f -> p (o f)"), start=k == 0,
                                 stop=k == HB - 1)
                    ins.then_inc(s_fy, 1)
                if here:
                    pe.wait_ge(s_fm, s + 1)
                    if st is None or st >= 1:
                        pe.wait_ge(s_fte, s)
                    for k in range(HB):
                        ins = tr(tp2[:, k * P:(k + 1) * P], hid[:, k:HID:HB])
                    ins.then_inc(s_fth, 1)

            slot_iterations(pe, slot)


INS = ["x", "adj", "L0_gnn_W", "L0_gnn_a", "L0_gnn_w_ih", "L0_gnn_w_hh", "L0_gnn_b_ih", "L0_gnn_b_hh",
       "L0_ffn_gate_w", "L0_ffn_gate_b", "L0_ffn_w1", "L0_ffn_w2", "L0_ffn_w3"]


def kernel(**inputs):
    import numpy as np
    import concourse.bacc as bacc
    from concourse.bass_utils import run_bass_kernel_spmd

    nc = bacc.Bacc("TRN2", target_bir_lowering=False, num_devices=1)
    arrays, args = {}, []
    for name in INS:
        v = np.ascontiguousarray(inputs[name])
        arrays["in_" + name] = v
        args.append(nc.dram_tensor("in_" + name, v.shape, mybir.dt.from_np(v.dtype), kind="ExternalInput").ap())
    n, f = inputs["x"].shape
    out = nc.dram_tensor("out", (n, f), F32, kind="ExternalOutput").ap()
    rows = nc.dram_tensor("token_rows", (n, f + 4), F32, kind="Internal").ap()
    gnn_moe(nc, *args, out, rows)
    return run_bass_kernel_spmd(nc, [arrays], core_ids=[0]).results[0]["out"]
```

```python
from contextlib import ExitStack

import concourse.bass as bass
from concourse import mybir

F32 = mybir.dt.float32
F32R = mybir.dt.float32r
BF16 = mybir.dt.bfloat16
I32 = mybir.dt.int32
U32 = mybir.dt.uint32
ACT = mybir.ActivationFunctionType
ALU = mybir.AluOpType
AX = mybir.AxisListType

P = 128
EPS = 1e-5
SLOPE = 0.2
DS = 1.0 / 256.0


def gnn_moe(nc, x, adj, W, a, w_ih, w_hh, b_ih, b_hh, gate_w, gate_b, w1, w2, w3, out, rows):
    N, F = x.shape
    T = N // P
    KB = F // P
    NE, _, HID = w1.shape
    HB = HID // P
    G3 = 3 * F
    VW = F + 2
    HC = 1024
    Q = N // HC
    MC = 512
    CPT = N // MC
    JB = MC // P
    CQ = HC // MC
    RW = F + 4
    SLOTS = (2 * N + NE * (P - 1)) // P
    WR = 4
    WB = 5


    ctx = ExitStack()
    with ctx:
        def sem(name):
            return ctx.enter_context(nc.semaphore(name))

        def sb(name, shape, dt, stack=ctx):
            return stack.enter_context(nc.sbuf_tensor(name, shape, dt))

        bank = [ctx.enter_context(nc.psum_tensor(f"bank{i}", [P, 512], F32)) for i in range(6)]
        pT = [ctx.enter_context(nc.psum_tensor(f"pT{i}", [P, 2 * MC], BF16)) for i in range(2)]
        accp, accm, rzb, nb, tp, tp2 = bank

        ident = sb("ident", [P, P], F32)
        identb = sb("identb", [P, P], BF16)
        onesf = sb("onesf", [P, P], F32)
        before = sb("before", [P, P], BF16)
        onesb = sb("onesb", [P, P], BF16)
        iota_e = sb("iota_e", [P, NE], F32)
        pick = sb("pick", [P, 2, T, NE], BF16)
        gbias = sb("gbias", [P, NE], F32)
        gwt = sb("gwt", [P, KB, NE], F32)

        gs = ExitStack()
        V = sb("V", [P, T, 4, VW], F32R, gs)
        Dp = sb("Dp", [P, N], F32, gs)
        adjb = sb("adjb", [P, Q, HC], BF16, gs)
        gbuf = sb("gbuf", [P, HC], BF16, gs)
        tbuf = sb("tbuf", [P, 2, HC], BF16, gs)
        mask = sb("mask", [P, 2, 2, MC], F32R, gs)
        wT = sb("wT", [P, 2, KB, G3], F32, gs)
        xin = sb("xin", [P, 4, F], F32, gs)
        xnb = sb("xnb", [P, 2, F], F32, gs)
        hT = sb("hT", [P, 2 * KB, P], F32, gs)
        scr = sb("scr", [P, 6 * F], F32, gs)
        comb = sb("comb", [P, VW], F32, gs)
        xrow = sb("xrow", [P, 2, RW], F32, gs)
        xn2T = sb("xn2T", [P, KB, P], F32, gs)
        bias_rz = sb("bias_rz", [P, 2 * F], F32, gs)
        bias_n = sb("bias_n", [P, 2 * F], F32, gs)
        xmv = sb("xmv", [P, T, 2], F32, gs)
        rstd = sb("rstd", [P, T], F32, gs)
        sd = sb("sd", [P, T, 2], F32, gs)
        BD = sb("BD", [P, T, 2], F32, gs)
        bst = sb("bst", [P, 4, 6], F32, gs)
        mv4 = sb("mv4", [P, 4, 2], F32, gs)
        mv = sb("mv", [P, 2], F32, gs)
        dmx = sb("dmx", [P, 2, Q], F32, gs)
        co = sb("co", [P, 2, 6], F32, gs)
        rden = sb("rden", [P, 1], F32, gs)
        var = sb("var", [P, 1], F32, gs)
        rs = sb("rs", [P, 1], F32, gs)
        mhalf = sb("mhalf", [P, 1], F32, gs)
        lg = sb("lg", [P, NE], F32, gs)
        top = sb("top", [P, 8], F32, gs)
        tix = sb("tix", [P, 8], U32, gs)
        rt = sb("rt", [P, 3], F32, gs)
        rz = scr[:, 0:2 * F]
        nn = scr[:, 2 * F:4 * F]
        hp = scr[:, 4 * F:5 * F]
        dd = scr[:, 5 * F:6 * F]
        wnat = scr[:, :].rearrange("p (r f) -> p r f", f=F)
        diag = scr[:, 0:4 * P].rearrange("p (t m) -> p t m", m=P)
        WXW = F + 3
        Wx = xrow[:, :, 0:WXW]
        xs = adjb[:, :, :].rearrange("p q c -> p (q c)")[:, 0:16 * F].bitcast(F32)\
            .rearrange("p (t f) -> p t f", f=F)
        thr = sd[:, :, 1]
        dbc = pT[0][:, :].bitcast(F32)
        x1 = xin[:, 2, :]
        a_row = bias_rz[:, :]
        bhh_rz = xin[:, 2:4, :].rearrange("p a f -> p (a f)")
        gs.close()

        fs = ExitStack()
        wexp = sb("wexp", [P, WB, 3, KB * HID], F32, fs)
        xg = sb("xg", [P, WR, RW], F32, fs)
        wup = sb("wup", [P, 2, 2, 2, KB * HID], F32R, fs)
        xT = sb("xT", [P, WR, 2, KB * P], F32R, fs)
        sil = sb("sil", [P, HID], F32, fs)
        hid = sb("hid", [P, HID], F32, fs)
        hidT = sb("hidT", [P, HB, P], F32, fs)
        ysc = sb("ysc", [P, WR, F], F32, fs)
        lanew = sb("lanew", [P, WR, 2], F32, fs)
        iota_q = sb("iota_q", [P, P], F32, fs)
        cnt = sb("cnt", [P, NE, T], F32, fs)
        scan = sb("scan", [P, NE, T], F32, fs)
        ones = sb("ones", [P, NE, T], F32, fs)
        posw = sb("posw", [P, T, NE], F32, fs)
        prod = sb("prod", [P, 2, T, NE], F32, fs)
        pos = sb("pos", [P, 2, T], F32, fs)
        posi = sb("posi", [P, 2, T], I32, fs)
        poss = sb("poss", [P, 2, T], I32, fs)
        sidx = sb("sidx", [P, 2, T], F32, fs)
        qidx = sb("qidx", [P, 2, T], F32, fs)
        tok = sb("tok", [P, T], F32, fs)
        r16 = sb("r16", [P, 8, NE], F32, fs)
        kio = sb("kio", [P, T], F32, fs)
        cmp1 = sb("cmp1", [P, NE, T], F32, fs)
        sio = sb("sio", [P, SLOTS + SLOTS % 2], F32, fs)
        cmp2 = sb("cmp2", [P, SLOTS, NE], F32, fs)
        esl = sb("esl", [P, SLOTS], F32, fs)
        esc = sb("esc", [P, SLOTS], F32, fs)
        fresh = sb("fresh", [P, SLOTS], F32, fs)
        order = sb("order", [P, SLOTS], F32, fs)
        ordi = sb("ordi", [P, 2, SLOTS], I32, fs)
        slot_tab = sb("slot_tab", [P, 3, SLOTS], I32, fs)
        sv = sb("sv", [P, SLOTS], F32, fs)
        gidx = sb("gidx", [P, SLOTS], U32, fs)
        cidx = sb("cidx", [P, SLOTS], U32, fs)
        gi1 = sb("gi1", [P, WR, 1], U32, fs)
        ci1 = sb("ci1", [P, WR, 1], U32, fs)
        assert N <= 4096
        lane_hot = sb("lane_hot", [P, 8, P], F32R, fs)
        slot_hot = sb("slot_hot", [P, 8, SLOTS + SLOTS % 2], F32R, fs)
        silu_warm = sb("silu_warm", [P, 1], F32, fs)
        fs.close()

        s_const = sem("constants_made")
        s_cld = sem("small_inputs_loaded")
        s_bld = sem("biases_loaded")
        s_wn = sem("gru_weights_loaded")
        s_wtr = sem("gru_weights_transposed")
        s_wev = sem("gru_weights_copied")
        s_wx = sem("W_extended")
        s_x = [sem(f"x_loaded{k}") for k in range(8)]
        s_var1 = sem("variance_of_x_done")
        s_rs1 = sem("deviation_of_x_done")
        s_var2 = sem("variance_of_x1_done")
        s_rs2 = sem("deviation_of_x1_done")
        s_xn = sem("xn_made")
        s_xt = sem("xn_transposed")
        s_xe = sem("xnT_copied")
        s_wh = sem("Wh_done")
        s_bd = sem("value_scales_done")
        s_hi = sem("value_hi_done")
        s_lo = sem("value_lo_done")
        s_dc = sem("d_diagonals_done")
        s_db = sem("d_broadcast")
        s_dpe = sem("d_broadcast_copied")
        s_vh = sem("denominator_hi_done")
        s_vd = sem("values_complete")
        s_link = sem("dve_link")
        s_adj = [sem(f"adj_loaded{q}") for q in range(Q)]
        s_t = sem("signed_adj_done")
        s_tr = sem("adj_transposed")
        s_mask = sem("masks_done")
        s_mm = sem("chunk_accumulated")
        s_nmx = sem("row_max_done")
        s_co = sem("row_scales_done")
        s_af = sem("accumulators_read")
        s_hp = sem("h_prime_done")
        s_xb = sem("xn_remade")
        s_th = sem("h_transposed")
        s_hT = sem("hT_copied")
        s_gru = sem("gru_products_done")
        s_rz = sem("rz_logits_done")
        s_gf = sem("gru_products_read")
        s_rzt = sem("rz_tanh_done")
        s_np = sem("n_logits_done")
        s_nt = sem("n_tanh_done")
        s_x1 = sem("x1_done")
        s_x1s = sem("x1_stored")
        s_xr = [sem(f"x_reloaded{u}") for u in range(2)]
        s_ln2 = sem("xn2_done")
        s_t2 = sem("xn2_transposed")
        s_t2e = sem("xn2T_copied")
        s_lgt = sem("gate_products_done")
        s_lg = sem("gate_logits_done")
        s_dl = sem("gate_difference_done")
        s_de = sem("gate_exp_done")
        s_row = sem("token_row_done")
        s_rows = [sem(f"token_row_stored{u}") for u in range(2)]
        s_rk = sem("ranks_done")
        s_io = sem("iotas_done")
        s_hot = sem("pair_one_hots_done")
        s_pl = sem("pair_placed")
        s_rd = sem("routing_done")
        s_tab = sem("slot_table_done")
        s_w = [sem(f"expert_weights_loaded{r}") for r in range(WR)]
        s_gc = sem("gather_index_copied")
        s_cc = sem("scatter_index_copied")
        s_g = [sem(f"tokens_gathered{r}") for r in range(WR)]
        s_sc = sem("outputs_added")
        s_lw = sem("lane_weights_done")
        s_ftx = sem("slot_tokens_transposed")
        s_fxe = sem("slot_tokensT_copied")
        s_fxl = sem("slot_tokensT_lo_done")
        s_whi = sem("up_weights_hi_done")
        s_wlo = sem("up_weights_lo_done")
        s_fh = sem("up_products_done")
        s_fs = sem("silu_done")
        s_fm = sem("hidden_done")
        s_fth = sem("hidden_transposed")
        s_fte = sem("hiddenT_copied")
        s_fy = sem("expert_outputs_done")
        s_fo = sem("weighted_outputs_done")

        block = ctx.enter_context(nc.Block())

        def tile_iterations(eng, body):
            for r in range(4):
                body(r, r, 0, r, 0)
            with eng.Fori(0, T // 8 - 1) as m:
                for n in range(1, 3):
                    for r in range(4):
                        body(m * 8 + (4 * n + r), r, m * 2 + n, None, n % 2)
            for i in range(T - 4, T + 4):
                body(i, i % 4, i // 4, i, i // 4 % 2)

        LAST = T + 3
        L0 = 4
        NL = (T - 1 - L0) // 2
        L1 = L0 + 2 * NL

        def graph_iterations(eng, body):
            for i in range(L0):
                body(i, i % 2, i // 2, i)
            with eng.Fori(0, NL) as m:
                for n in range(2):
                    body(m * 2 + (L0 + n), (L0 + n) % 2, m + (L0 + n) // 2, None)
            for i in range(L1, LAST):
                body(i, i % 2, i // 2, i)

        def live(static, lag):
            return static is None or 0 <= static - lag < T

        def after(static, lag, n):
            return static is None or static - lag >= n

        def pair_iterations(eng, body):
            for k in range(8):
                body(k // 2, k % 2, k, k // 2)
            with eng.Fori(1, T // 4 - 1) as m:
                for k in range(8):
                    body(m * 4 + k // 2, k % 2, k, None)
            for k in range(8):
                body(T - 4 + k // 2, k % 2, k, T - 4 + k // 2)

        FULL = (SLOTS - 2) // WR

        def slot_iterations(eng, body):
            for s in range(2 * WR):
                body(s, s % WR, s // WR, s)
            with eng.Fori(2, FULL) as m:
                for r in range(WR):
                    body(m * WR + r, r, m, None)
            for s in range(FULL * WR, SLOTS + 1):
                body(s, s % WR, s // WR, s)

        def at(t, size=1):
            return slice(t, t + size) if isinstance(t, int) else bass.ds(t, size)

        EXPERT, NEW, BUF = range(3)

        def table(eng, k, s):
            return eng.value_load(slot_tab[0:1, k, at(s)], min_val=0, max_val=(NE - 1, 1, WB - 1)[k])

        def one(b):
            return bass.ds(b, 1)

        def wh_bank(r):
            return (rzb, nb, accp, accm)[r % 4]

        def wait_apart(eng, *waits):
            held = [(semaphore, v if isinstance(v, int) else eng.to_reg(v)) for semaphore, v in waits]
            eng.wait_ge(s_const, CONSTS)
            for semaphore, v in held:
                eng.wait_ge(semaphore, v)

        CONSTS = 10
        @block.sync
        def _(sp):
            row = lambda b, lo, hi: b[lo:hi].rearrange("(o f) -> o f", o=1).broadcast_to([P, hi - lo])
            sp.dma_start(Wx[:, :, 0:F], W.rearrange("(k p) f -> p k f", p=P)).then_inc(s_cld, 16)
            sp.dma_start(a_row, a.rearrange("f o -> o f").broadcast_to([P, 2 * F])).then_inc(s_cld, 16)
            sp.dma_start(gwt[:, :, :], gate_w.rearrange("(k p) e -> p k e", p=P)).then_inc(s_cld, 16)
            sp.dma_start(gbias[:, :], row(gate_b, 0, NE)).then_inc(s_cld, 16)
            sp.dma_start(wnat, w_ih.rearrange("(r p) f -> p r f", p=P)).then_inc(s_wn, 16)
            groups = x.rearrange("(t p) f -> p t f", p=P)
            for k in range(8):
                sp.dma_start(xs[:, k, :], x[k * P:(k + 1) * P, :]).then_inc(s_x[k], 16)
            sp.wait_ge(s_wx, 3 * KB)
            sp.dma_start(bias_rz[:, :], row(b_ih, 0, 2 * F)).then_inc(s_bld, 16)
            sp.dma_start(bhh_rz, row(b_hh, 0, 2 * F)).then_inc(s_bld, 16)
            sp.dma_start(bias_n[:, 0:F], row(b_ih, 2 * F, 3 * F)).then_inc(s_bld, 16)
            sp.dma_start(bias_n[:, F:2 * F], row(b_hh, 2 * F, 3 * F)).then_inc(s_bld, 16)
            with sp.Fori(1, T // 8) as g:
                for k in range(8):
                    sp.wait_ge(s_xn, g * 8 + (k - 7))
                    sp.dma_start(xs[:, k, :], x[bass.ds((g * 8 + k) * P, P), :]).then_inc(s_x[k], 16)

            def body(i, u, h, st):
                if live(st, 1):
                    if after(st, 1, 2):
                        sp.wait_ge(s_x1, i - 2)
                    sp.dma_start(xin[:, (u + 1) % 2, :], x[at((i - 1) * P, P), :]).then_inc(s_xr[(u + 1) % 2], 16)
                if live(st, 2):
                    sp.wait_ge(s_x1, i - 1)
                    sp.dma_start(out[at((i - 2) * P, P), :], x1).then_inc(s_x1s, 16)
                if live(st, 3):
                    sp.wait_ge(s_row, i - 2)
                    sp.dma_start(rows[at((i - 3) * P, P), :], xrow[:, (u + 1) % 2, :]).then_inc(s_rows[(u + 1) % 2], 16)

            graph_iterations(sp, body)

            w1v, w2v = (w.rearrange("e (p k) h -> e p (k h)", k=KB) for w in (w1, w2))
            w3v = w3.rearrange("e (p k) o -> e p (k o)", k=HB)
            sp.wait_ge(s_tab, 3)

            def load(s, r, m, st):
                if st == SLOTS:
                    return
                e, new, b = (table(sp, k, s) for k in (EXPERT, NEW, BUF))
                waits = []
                if st is None or st >= WR:
                    waits.append((s_whi, s * 2 + (1 - 2 * WR)))
                if st is None or st >= WB:
                    waits.append((s_fy, s - (WB - 1)))
                if waits:
                    wait_apart(sp, *waits)
                for n, wv in enumerate((w1v, w2v, w3v)):
                    sp.dma_start(wexp[:, one(b), n, :].rearrange("p o f -> p (o f)"),
                                 wv[one(e), :, :].rearrange("o p f -> (o p) f"), cond=new == 1).then_inc(s_w[r], 16)

            slot_iterations(sp, load)
            sp.wait_ge(s_sc, 16 * SLOTS)

        @block.gpsimd
        def _(pool):
            def load_adj(t, q):
                pool.dma_start(adjb[:, q, :], adj[at(t * P, P), q * HC:(q + 1) * HC]).then_inc(s_adj[q], 16)

            nc.gpsimd.memset(ident[:], 0.0).then_inc(s_const, 1)
            nc.gpsimd.memset(before[:], 1.0).then_inc(s_const, 1)
            nc.gpsimd.memset(onesb[:], 1.0).then_inc(s_const, 1)
            nc.gpsimd.memset(onesf[:], 1.0).then_inc(s_const, 1)
            nc.gpsimd.memset(mhalf[:], -0.5).then_inc(s_const, 1)
            nc.gpsimd.memset(V[:, :, :, F + 1:F + 2].bitcast(F32), 0.0).then_inc(s_const, 1)
            nc.gpsimd.iota(iota_e[:], [[1, NE]], base=0, channel_multiplier=0,
                           allow_small_or_imprecise_dtypes=True).then_inc(s_const, 1)
            pool.wait_ge(s_const, 7)
            nc.gpsimd.affine_select(out=ident[:], in_=ident[:], compare_op=ALU.not_equal, fill=1.0, base=0,
                                    pattern=[[-1, P]], channel_multiplier=1).then_inc(s_const, 1)
            nc.gpsimd.affine_select(out=before[:], in_=before[:], compare_op=ALU.is_gt, fill=0.0, base=0,
                                    pattern=[[1, P]], channel_multiplier=-1).then_inc(s_const, 1)
            pool.wait_ge(s_const, 9)
            nc.gpsimd.tensor_copy(identb[:], ident[:]).then_inc(s_const, 1)
            with pool.Fori(0, T // 4) as g:
                wait_apart(pool, (s_var1, g + 1))
                dev = rstd[:, at(g * 4, 4)]
                nc.gpsimd.tensor_tensor(dev, dev, mhalf[:, :].broadcast_to([P, 4]), ALU.pow).then_inc(s_rs1, 1)
            for q in range(Q):
                pool.wait_ge(s_xn, T - 8 + (q + 1) * 8 // Q)
                load_adj(0, q)

            def body(i, u, h, st):
                if st is None or st + 1 < T:
                    for q in range(Q):
                        pool.wait_ge(s_t, i * Q + (q + 1))
                        load_adj(i + 1, q)
                if live(st, 2):
                    pool.wait_ge(s_var2, i - 1)
                    nc.gpsimd.tensor_tensor(rs[:, :], var[:, :], mhalf[:, :], ALU.pow).then_inc(s_rs2, 1)

            graph_iterations(pool, body)

            pool.wait_ge(s_mm, T * CPT)
            pool.wait_ge(s_t, T * Q)
            imp = dict(allow_small_or_imprecise_dtypes=True)
            nc.gpsimd.iota(sio[:], [[1, SLOTS + SLOTS % 2]], base=0, channel_multiplier=0, **imp).then_inc(s_io, 1)
            nc.gpsimd.iota(kio[:], [[P, T]], base=0, channel_multiplier=0, **imp).then_inc(s_io, 1)
            nc.gpsimd.iota(iota_q[:], [[1, P]], base=0, channel_multiplier=0, **imp).then_inc(s_io, 1)
            nc.gpsimd.iota(tok[:], [[P, T]], base=1, channel_multiplier=1, **imp).then_inc(s_io, 1)
            nc.gpsimd.memset(ones[:], 1.0).then_inc(s_io, 1)

            def gather(s, r, m, st):
                if st is None or st >= WR:
                    pool.wait_ge(s_lw, s - (WR - 1))
                    pool.wait_ge(s_ftx, s - (WR - 1))
                nc.gpsimd.tensor_copy(gi1[:, r, :], gidx[:, at(s)]).then_inc(s_gc, 1)
                wait_apart(pool, (s_gc, s + 1))
                nc.gpsimd.indirect_dma_start(
                    out=xg[:, r, :], out_offset=None, in_=rows[:, :],
                    in_offset=bass.IndirectOffsetOnAxis(ap=gi1[:, r, :], axis=0)).then_inc(s_g[r], 16)

            def scatter(s, r, m, st):
                nc.gpsimd.tensor_copy(ci1[:, r, :], cidx[:, at(s)]).then_inc(s_cc, 1)
                waits = [(s_cc, s + 1), (s_fo, s + 1)]
                if st is None or st >= 1:
                    waits.append((s_sc, s * 16))
                wait_apart(pool, *waits)
                nc.gpsimd.indirect_dma_start(
                    out=out[:, :], out_offset=bass.IndirectOffsetOnAxis(ap=ci1[:, r, :], axis=0),
                    in_=ysc[:, r, :], in_offset=None, compute_op=ALU.add,
                    bounds_check=N - 1, oob_is_err=False).then_inc(s_sc, 16)

            for par in range(2):
                pool.wait_ge(s_rows[par], 16 * (T // 2))
            pool.wait_ge(s_x1s, 16 * T)
            pool.wait_ge(s_rd, 2)
            gather(0, 0, 0, 0)
            gather(1, 1, 0, 1)

            def slot(s, r, m, st):
                if st is None or st + 2 < SLOTS:
                    gather(s + 2, (r + 2) % WR, m + (r + 2) // WR, None if st is None else st + 2)
                if st is None or st >= 1:
                    scatter(s - 1, (r - 1) % WR, m + (r - 1) // WR, None if st is None else st - 1)

            slot_iterations(pool, slot)

        @block.scalar
        def _(act):
            act_copy = lambda o, i: nc.scalar.activation(o, i, ACT.Copy)

            def copy_gru_weights(m):
                for n in range(2 * KB):
                    kb, half = n // 2, n % 2
                    act.wait_ge(s_wtr, 2 * KB * m + n + 1)
                    act_copy(wT[:, m, kb, half * 3 * P:(half + 1) * 3 * P],
                             (accp, accm)[n % 2][:, 0:3 * P]).then_inc(s_wev, 1)

            copy_gru_weights(0)
            act.dma_start(wnat, w_hh.rearrange("(r p) f -> p r f", p=P)).then_inc(s_wn, 16)
            copy_gru_weights(1)

            def values(i, r, g, st, par):
                if live(st, 1):
                    act.wait_ge(s_wh, i)
                    nc.scalar.activation(BD[:, at(i - 1), :], wh_bank(r - 1)[:, F:F + 2], ACT.Exp).then_inc(s_bd, 1)
                if live(st, 0):
                    act.wait_ge(s_xt, i + 1)
                    if after(st, 0, 2):
                        act.wait_ge(s_wh, i - 1)
                    p = r % 2
                    act_copy(hT[:, KB * p:KB * p + KB, :].rearrange("p k m -> p (k m)"),
                             (tp, tp2)[p][:, 0:F]).then_inc(s_xe, 1)
                if live(st, 1):
                    act.wait_ge(s_bd, i)
                    for k in range(2):
                        nc.scalar.activation(V[:, at(i - 1), 2 * k, 0:F], wh_bank(r - 1)[:, 0:F], ACT.Copy,
                                             scale=BD[:, at(i - 1), k]).then_inc(s_hi, 1)
                if r == 3 and (st is None or st > 3):
                    act.wait_ge(s_db, g)
                    act_copy(Dp[:, at((g - 1) * 4 * P, 4 * P)], dbc).then_inc(s_dpe, 1)

            tile_iterations(act, values)
            for k in range(2):
                act_copy(V[:, :, 2 * k, F], BD[:, :, k]).then_inc(s_vh, 1)

            def masks(i, c, st):
                C = i * CPT + c
                act.wait_ge(s_tr, C + 1)
                if st is None or st * CPT + c >= 2:
                    act.wait_ge(s_mm, C - 1)
                for k, sign in enumerate((2.0, -2.0)):
                    ins = nc.scalar.activation(mask[:, c % 2, k, :], pT[c % 2][:, 0:MC], ACT.Relu, scale=sign)
                ins.then_inc(s_mask, 1)

            masks(0, 0, 0)

            def rz_tanh(i, u):
                act.wait_ge(s_rz, i - 1)
                nc.scalar.activation(rz, rz, ACT.Tanh, scale=0.5).then_inc(s_rzt, 1)

            def n_tanh(i, u):
                act.wait_ge(s_np, i - 1)
                nc.scalar.activation(nn[:, 0:F], nn[:, 0:F], ACT.Tanh).then_inc(s_nt, 1)

            def copy_hT(i, u, st):
                act.wait_ge(s_th, i)
                if after(st, 1, 1):
                    act.wait_ge(s_gru, i - 1)
                act_copy(hT[:, :, :].rearrange("p k m -> p (k m)"), tp[:, :]).then_inc(s_hT, 1)

            def gate_exp(i, u):
                act.wait_ge(s_dl, i - 2)
                nc.scalar.activation(rt[:, 1:2], rt[:, 0:1], ACT.Exp).then_inc(s_de, 1)

            def row_scales(i, u):
                act.wait_ge(s_nmx, i + 1)
                for k, slope in enumerate((1.0, SLOPE)):
                    ins = nc.scalar.activation(co[:, u, k:k + 1], thr[:, at(i)], ACT.Exp, scale=-slope / DS,
                                               bias=co[:, u, 5:6])
                ins.then_inc(s_co, 1)

            def body(i, u, h, st):
                for c in range(CPT):
                    if c and live(st, 0):
                        masks(i, c, st)
                    if c == 0 and live(st, 3):
                        act.wait_ge(s_t2, i - 2)
                        act_copy(xn2T[:, :, :].rearrange("p k m -> p (k m)"), tp2[:, 0:F]).then_inc(s_t2e, 1)
                    if c == 1 and live(st, 2):
                        rz_tanh(i, u)
                    if c == min(3, CPT - 1) and live(st, 1):
                        copy_hT(i, u, st)
                    if c == min(4, CPT - 1):
                        if live(st, 2):
                            n_tanh(i, u)
                        if live(st, 3):
                            gate_exp(i, u)
                    if c == min(6, CPT - 1) and live(st, 0):
                        row_scales(i, u)
                if st is None or st + 1 < T:
                    masks(i + 1, 0, None if st is None else st + 1)

            graph_iterations(act, body)

            def copy_slot_xT(s, r, st):
                act.wait_ge(s_ftx, s + 1)
                if st is None or st >= WR:
                    act.wait_ge(s_fh, (s - (WR - 1)) * 2)
                act_copy(xT[:, r, 0, :], tp[:, 0:F]).then_inc(s_fxe, 1)

            def split_hi(s, r, m, st, b, n):
                waits = []
                if n == 0:
                    waits.append((s_w[r], m * 48 + 48))
                if st is None or st >= 2:
                    waits.append((s_fh, s * 2 + (n - 3)))
                if waits:
                    wait_apart(act, *waits)
                act_copy(wup[:, r % 2, n, 0, :], wexp[:, one(b), n, :].rearrange("p o f -> p (o f)")).then_inc(s_whi, 1)

            act.wait_ge(s_tab, 3)
            nc.scalar.activation(silu_warm[:, :], iota_e[:, 0:1], ACT.Silu)
            for k in range(2):
                b = table(act, BUF, k)
                for n in range(2):
                    split_hi(k, k, 0, k, b, n)
                if k == 0:
                    copy_slot_xT(0, 0, 0)

            def slot(s, r, m, st):
                if st == SLOTS:
                    return
                two_on = st is None or st + 2 < SLOTS
                ahead = (s + 2, (r + 2) % WR, m + (r + 2) // WR, None if st is None else st + 2)
                if two_on:
                    b = table(act, BUF, s + 2)
                act.wait_ge(s_fh, s * 2 + 1)
                if st is None or st >= 1:
                    act.wait_ge(s_fm, s)
                nc.scalar.activation(sil[:, :], rzb[:, :], ACT.Silu).then_inc(s_fs, 1)
                if two_on:
                    split_hi(*ahead, b, 0)
                if st is None or st + 1 < SLOTS:
                    copy_slot_xT(s + 1, (r + 1) % WR, None if st is None else st + 1)
                if two_on:
                    split_hi(*ahead, b, 1)
                act.wait_ge(s_fth, s + 1)
                if st is None or st >= 1:
                    act.wait_ge(s_fy, s)
                act_copy(hidT[:, :, :].rearrange("p k m -> p (k m)"), tp2[:, :]).then_inc(s_fte, 1)

            slot_iterations(act, slot)

        @block.vector
        def _(dve):
            V_ = nc.vector
            done = [0]

            def link(ins, alone=False):
                done[0] = done[0] + 1
                ins.then_inc(s_link, 1)
                if alone:
                    wait_apart(dve, (s_link, done[0]))
                else:
                    dve.wait_ge(s_link, done[0])

            dve.wait_ge(s_cld, 64)
            for kb in range(KB):
                for n, (half, scale) in enumerate(((1, 1.0), (1, SLOPE), (0, -1.0))):
                    V_.tensor_tensor_reduce(out=comb[:, 0:F], in0=Wx[:, kb, 0:F], in1=a_row[:, half * F:half * F + F],
                                            scale=scale, scalar=0.0, op0=ALU.mult, op1=ALU.add,
                                            accum_out=Wx[:, kb, F + n:F + n + 1]).then_inc(s_wx, 1)
                    dve.wait_ge(s_wx, 3 * kb + n + 1)

            def deviation_in(g):
                V_.tensor_scalar(rstd[:, at(g * 4, 4)], mv4[:, :, 1], EPS, None, ALU.add).then_inc(s_var1, 1)
                link(V_.tensor_copy(xmv[:, at(g * 4, 4), :], mv4[:, :, :]))

            for r in range(4):
                dve.wait_ge(s_x[r], 16)
                ins = V_.bn_stats(bst[:, r, :], xs[:, r, :])
            link(ins)
            for r in range(4):
                ins = V_.bn_aggr(mv4[:, r, :], bst[:, r, :])
            link(ins)
            deviation_in(0)

            def moments(src, var_done):
                link(V_.bn_stats(bst[:, 0, :], src), True)
                link(V_.bn_aggr(mv[:, :], bst[:, 0, :]))
                V_.tensor_scalar(var[:, :], mv[:, 1:2], EPS, None, ALU.add).then_inc(var_done, 1)

            first_links = done[0]
            GROUP_LINKS = 7

            def links_before(g, r):
                if isinstance(g, int) and g == 0:
                    return first_links + r
                if isinstance(g, int) and g == T // 4:
                    return first_links + (g - 1) * GROUP_LINKS + (r > 1)
                stats = r if not isinstance(g, int) or g < T // 4 - 1 else 0
                return g * GROUP_LINKS + (first_links - 1 + stats + (r > 1))

            def values(i, r, g, st, par):
                done[0] = links_before(g, r)
                ahead = st is None or st + 4 < T
                if ahead:
                    k = (1 - par) * 4 + r
                    turn = (st + 4) // 8 if st is not None else (i - r - 4 * par) // 8 + par
                    dve.wait_ge(s_x[k], turn * 16 + 16)
                    V_.bn_stats(bst[:, r, :], xs[:, k, :]).then_inc(s_link, 1)
                    done[0] = done[0] + 1
                    stats_done = done[0]
                if live(st, 0):
                    if r == 0:
                        dve.wait_ge(s_rs1, g + 1)
                    if after(st, 0, 2):
                        dve.wait_ge(s_xt, i - 1)
                    V_.tensor_scalar(xnb[:, r % 2, :], xs[:, par * 4 + r, :], xmv[:, at(i), 0:1], rstd[:, at(i)], ALU.subtract,
                                     ALU.mult).then_inc(s_xn, 1)
                if live(st, 2):
                    wh = wh_bank(r - 2)
                    dve.wait_ge(s_hi, (i - 1) * 2)
                    columns = V_.tensor_scalar(sd[:, at(i - 2), :], wh[:, F:F + 3:2], DS, None, ALU.mult)
                    if r == 1:
                        link(columns)
                    for k in range(2):
                        V_.scalar_tensor_tensor(out=V[:, at(i - 2), 2 * k + 1, 0:F], in0=wh[:, 0:F],
                                                scalar=BD[:, at(i - 2), k], in1=V[:, at(i - 2), 2 * k, 0:F].bitcast(F32),
                                                op0=ALU.mult, op1=ALU.subtract).then_inc(s_lo, 1)
                if r == 1 and (st is None or st > 1):
                    V_.tensor_tensor(diag[:, :, :], ident[:, :].unsqueeze(1).broadcast_to([P, 4, P]),
                                     sd[:, at((g - 1) * 4, 4), 0:1].broadcast_to([P, 4, P]), ALU.mult).then_inc(s_dc, 1)
                if ahead:
                    wait_apart(dve, (s_link, stats_done))
                    ins = V_.bn_aggr(mv4[:, r, :], bst[:, r, :])
                    if r == 3:
                        link(ins)
                        deviation_in(g + 1)

            tile_iterations(dve, values)
            done[0] = links_before(T // 4, 3)
            def piece(i, q, u, st):
                waits = [(s_adj[q], i * 16 + 16)]
                if st == 0:
                    waits.append((s_dpe, (q + 1) * HC // (4 * P)))
                if st is None or st or q:
                    waits.append((s_t, i * Q + q))
                wait_apart(dve, *waits)
                cols = slice(q * HC, (q + 1) * HC)
                link(V_.tensor_tensor_reduce(out=gbuf[:, :], in0=Dp[:, cols], in1=adjb[:, q, :], scale=1.0, scalar=-1e30,
                                             op0=ALU.add, op1=ALU.max, accum_out=dmx[:, u, q:q + 1]))
                link(V_.tensor_scalar(gbuf[:, :], Dp[:, cols], thr[:, at(i)], 0.5, ALU.is_gt, ALU.subtract))
                if st is None or st * Q + q >= 2:
                    dve.wait_ge(s_tr, (i * Q + (q - 1)) * CQ)
                V_.tensor_tensor(tbuf[:, q % 2, :], adjb[:, q, :], gbuf[:, :], ALU.mult).then_inc(s_t, 1)

            def row_max(i, u):
                c = lambda k: co[:, u, k:k + 1]
                link(V_.tensor_reduce(c(2), dmx[:, u, :], AX.X, ALU.max))
                link(V_.tensor_scalar(c(3), c(2), 1.0, thr[:, at(i)], ALU.subtract, ALU.subtract))
                link(V_.tensor_scalar(c(4), c(3), -SLOPE / DS, None, ALU.mult))
                V_.scalar_tensor_tensor(out=c(5), in0=c(3), scalar=-1.0 / DS, in1=c(4), op0=ALU.mult,
                                        op1=ALU.min).then_inc(s_nmx, 1)

            def combine(i, u, st):
                v = (u + 1) % 2
                dve.wait_ge(s_mm, i * CPT)
                dve.wait_ge(s_co, i)
                link(V_.tensor_scalar(comb[:, 0:F + 1], accm[:, 0:F + 1], co[:, v, 1:2], None, ALU.mult))
                V_.scalar_tensor_tensor(out=comb[:, 0:F + 1], in0=accp[:, 0:F + 1], scalar=co[:, v, 0:1],
                                        in1=comb[:, 0:F + 1], op0=ALU.mult, op1=ALU.add).then_inc(s_af, 1)
                dve.wait_ge(s_af, i)
                link(V_.reciprocal(rden[:, :], comb[:, F:F + 1]))
                if after(st, 1, 1):
                    dve.wait_ge(s_th, i - 1)
                V_.tensor_scalar(hp, comb[:, 0:F], rden[:, 0:1], None, ALU.mult).then_inc(s_hp, 1)

            def remake_xn(i, u, h, st):
                v = (u + 1) % 2
                dve.wait_ge(s_xr[v], (h + (u - 1) // 2) * 16 + 16)
                V_.tensor_scalar(xnb[:, v, :], xin[:, v, :], xmv[:, at(i - 1), 0:1], rstd[:, at(i - 1)], ALU.subtract,
                                 ALU.mult).then_inc(s_xb, 1)

            def gru_logits(i):
                dve.wait_ge(s_gru, i - 1)
                V_.tensor_tensor(rz, rzb[:, :], bias_rz[:, :], ALU.add).then_inc(s_rz, 1)
                V_.tensor_tensor(nn, nb[:, :], bias_n[:, :], ALU.add).then_inc(s_gf, 1)

            def gru_n(i):
                dve.wait_ge(s_rzt, i - 1)
                dve.wait_ge(s_gf, i - 1)
                link(V_.scalar_tensor_tensor(out=nn[:, F:2 * F], in0=rz[:, 0:F], scalar=1.0, in1=nn[:, F:2 * F],
                                             op0=ALU.add, op1=ALU.mult))
                V_.scalar_tensor_tensor(out=nn[:, 0:F], in0=nn[:, F:2 * F], scalar=0.5, in1=nn[:, 0:F], op0=ALU.mult,
                                        op1=ALU.add).then_inc(s_np, 1)

            def gru_out(i, u, st):
                dve.wait_ge(s_nt, i - 1)
                link(V_.tensor_tensor(dd, xnb[:, u, :], nn[:, 0:F], ALU.subtract))
                link(V_.scalar_tensor_tensor(out=dd, in0=rz[:, F:2 * F], scalar=1.0, in1=dd, op0=ALU.add, op1=ALU.mult))
                link(V_.scalar_tensor_tensor(out=dd, in0=dd, scalar=0.5, in1=nn[:, 0:F], op0=ALU.mult, op1=ALU.add))
                if after(st, 2, 1):
                    dve.wait_ge(s_x1s, (i - 2) * 16)
                V_.tensor_tensor(x1, dd, xin[:, u, :], ALU.add).then_inc(s_x1, 1)

            def norm2(i, u, h, st):
                dve.wait_ge(s_x1, i - 1)
                moments(x1, s_var2)
                dve.wait_ge(s_rs2, i - 1)
                if after(st, 2, 2):
                    dve.wait_ge(s_rows[u], (h + (u - 4) // 2) * 16 + 16)
                V_.tensor_scalar(xrow[:, u, 0:F], x1, mv[:, 0:1], rs[:, 0:1], ALU.subtract, ALU.mult).then_inc(s_ln2, 1)

            def route_top(i, u):
                v = (u + 1) % 2
                dve.wait_ge(s_lgt, i - 2)
                V_.tensor_tensor(lg[:, :], tp2[:, F:F + NE], gbias[:, :], ALU.add).then_inc(s_lg, 1)
                wait_apart(dve, (s_lg, i - 2))
                link(V_.max(top[:, :], lg[:, :]))
                V_.tensor_tensor(rt[:, 0:1], top[:, 1:2], top[:, 0:1], ALU.subtract).then_inc(s_dl, 1)
                link(V_.max_index(tix[:, :], top[:, :], lg[:, :]))
                link(V_.tensor_copy(xrow[:, v, F + 2:F + 4], tix[:, 0:2]))
                for k in range(2):
                    V_.tensor_scalar(pick[:, k, at(i - 3), :], iota_e[:, :], xrow[:, v, F + 2 + k:F + 3 + k], None,
                                     ALU.is_equal)

            def route_weights(i, u):
                v = (u + 1) % 2
                dve.wait_ge(s_de, i - 2)
                link(V_.tensor_scalar(rt[:, 2:3], rt[:, 1:2], 1.0, None, ALU.add))
                link(V_.reciprocal(xrow[:, v, F:F + 1], rt[:, 2:3]))
                V_.tensor_tensor(xrow[:, v, F + 1:F + 2], rt[:, 1:2], xrow[:, v, F:F + 1], ALU.mult).then_inc(s_row, 1)

            piece(0, 0, 0, 0)
            for k in range(2):
                dve.wait_ge(s_vh, k + 1)
                V_.tensor_tensor(V[:, :, 2 * k + 1, F], BD[:, :, k], V[:, :, 2 * k, F].bitcast(F32),
                                 ALU.subtract).then_inc(s_vd, 1)
            dve.wait_ge(s_bld, 64)
            link(V_.tensor_tensor(bias_rz[:, :], bias_rz[:, :], bhh_rz, ALU.add))
            loop_links = [None, None]
            ITER_LINKS = 2 * Q + 3 + 2 + 1 + 3 + 2 + 3 + 2

            def body(i, u, h, st):
                if st is None:
                    if loop_links[0] is None:
                        loop_links[0] = done[0]
                    done[0] = loop_links[0] + (i - L0) * ITER_LINKS
                elif loop_links[0] is not None and st == L1:
                    done[0] = loop_links[0] + (L1 - L0) * ITER_LINKS
                start = done[0]
                if live(st, 1):
                    combine(i, u, st)
                    remake_xn(i, u, h, st)
                if live(st, 0) and Q > 1:
                    piece(i, 1, u, st)
                if live(st, 2):
                    gru_logits(i)
                if live(st, 0) and Q > 2:
                    piece(i, 2, u, st)
                if live(st, 2):
                    gru_n(i)
                if live(st, 3):
                    route_top(i, u)
                if live(st, 0):
                    for q in range(3, Q):
                        piece(i, q, u, st)
                if live(st, 2):
                    gru_out(i, u, st)
                if live(st, 0):
                    row_max(i, u)
                if live(st, 3):
                    route_weights(i, u)
                if st is None or st + 1 < T:
                    piece(i + 1, 0, (u + 1) % 2, None if st is None else st + 1)
                if live(st, 2):
                    norm2(i, u, h, st)
                if st is not None and L0 <= st < T - 1:
                    assert done[0] - start == ITER_LINKS, (done[0] - start, ITER_LINKS)

            graph_iterations(dve, body)

            dve.wait_ge(s_rk, 2)
            dve.wait_ge(s_io, 5)
            R = lambda k: r16[:, k, :]
            per_t = lambda v: v.unsqueeze(2).broadcast_to([P, NE, T])
            total, tiles, tend, tstart, tincl, estart, base = (R(k) for k in range(7))
            link(V_.tensor_copy(cnt[:, :, :], nb[:, 0:T * NE].rearrange("p (t e) -> p e t", e=NE)))
            link(V_.tensor_reduce(total, cnt[:, :, :], AX.X, ALU.add))
            flat = lambda v: v.rearrange("p e t -> p (e t)")
            link(V_.tensor_tensor_scan(flat(scan[:, :, :]), flat(ones[:, :, :]), flat(cnt[:, :, :]), 0.0, ALU.mult, ALU.add))
            link(V_.tensor_tensor(cmp1[:, :, :], per_t(total), kio[:, :].unsqueeze(1).broadcast_to([P, NE, T]), ALU.is_gt))
            link(V_.tensor_reduce(tiles, cmp1[:, :, :], AX.X, ALU.add))
            link(V_.tensor_tensor_scan(tend, ones[:, 0, 0:NE], tiles, 0.0, ALU.mult, ALU.add))
            link(V_.tensor_tensor_scan(tincl, ones[:, 0, 0:NE], total, 0.0, ALU.mult, ALU.add))
            link(V_.tensor_tensor(tstart, tend, tiles, ALU.subtract))
            link(V_.tensor_tensor(estart, tincl, total, ALU.subtract))
            link(V_.scalar_tensor_tensor(out=base, in0=tstart, scalar=float(P), in1=estart, op0=ALU.mult, op1=ALU.subtract))
            link(V_.tensor_tensor(cmp1[:, :, :], scan[:, :, :], cnt[:, :, :], ALU.subtract))
            link(V_.tensor_tensor(cmp1[:, :, :], cmp1[:, :, :], per_t(base), ALU.add))
            link(V_.tensor_tensor(posw[:, :, :].rearrange("p t e -> p e t"), cmp1[:, :, :],
                                  rzb[:, 0:T * NE].rearrange("p (t e) -> p e t", e=NE), ALU.add))
            for k in range(2):
                link(V_.tensor_tensor(prod[:, k, :, :], pick[:, k, :, :], posw[:, :, :], ALU.mult))
            link(V_.tensor_reduce(pos[:, :, :].rearrange("p k t -> p (k t)"),
                                  prod[:, :, :, :].rearrange("p k t e -> p (k t) e"), AX.X, ALU.add))
            link(V_.tensor_copy(posi[:, :, :], pos[:, :, :]))
            link(V_.tensor_single_scalar(poss[:, :, :], posi[:, :, :], P.bit_length() - 1, ALU.arith_shift_right))
            link(V_.tensor_copy(sidx[:, :, :], poss[:, :, :]))
            link(V_.scalar_tensor_tensor(out=qidx[:, :, :], in0=sidx[:, :, :], scalar=-float(P), in1=pos[:, :, :],
                                         op0=ALU.mult, op1=ALU.add))

            link(V_.tensor_tensor(cmp2[:, :, :], sio[:, 0:SLOTS].unsqueeze(2).broadcast_to([P, SLOTS, NE]),
                                  tend.unsqueeze(1).broadcast_to([P, SLOTS, NE]), ALU.is_ge))
            link(V_.tensor_reduce(esc[:, :], cmp2[:, :, :], AX.X, ALU.add))
            link(V_.tensor_scalar(esl[:, :], esc[:, :], float(NE - 1), None, ALU.min))
            V_.tensor_copy(slot_tab[:, EXPERT, :], esl[:, :]).then_inc(s_tab, 1)
            link(V_.tensor_copy(fresh[:, 0:1], ones[:, 0, 0:1]))
            link(V_.tensor_tensor(fresh[:, 1:SLOTS], esl[:, 1:SLOTS], esl[:, 0:SLOTS - 1], ALU.not_equal))
            V_.tensor_copy(slot_tab[:, NEW, :], fresh[:, :]).then_inc(s_tab, 1)
            link(V_.tensor_tensor_scan(order[:, :], flat(ones[:, :, :])[:, 0:SLOTS], fresh[:, :], 0.0, ALU.mult, ALU.add))
            assert all(n * 13 >> 6 == n // WB for n in range(NE + 1))
            link(V_.tensor_scalar(esc[:, :], order[:, :], 13.0, None, ALU.mult))
            link(V_.tensor_copy(ordi[:, 0, :], esc[:, :]))
            link(V_.tensor_single_scalar(ordi[:, 1, :], ordi[:, 0, :], 6, ALU.arith_shift_right))
            link(V_.tensor_copy(esc[:, :], ordi[:, 1, :]))
            V_.scalar_tensor_tensor(out=slot_tab[:, BUF, :], in0=esc[:, :], scalar=-float(WB), in1=order[:, :],
                                    op0=ALU.mult, op1=ALU.add).then_inc(s_tab, 1)

            def pair(t, k, b, st):
                n = t * 2 + k
                if b % 4 == 0:
                    if st is None or st >= 4:
                        dve.wait_ge(s_pl, n - 4)
                    V_.tensor_tensor(lane_hot[:, b:b + 4, :].rearrange("p (t k) m -> p t k m", k=2),
                                     iota_q[:, :].unsqueeze(1).unsqueeze(1).broadcast_to([P, 2, 2, P]),
                                     qidx[:, :, at(t, 2)].rearrange("p k t -> p t k").unsqueeze(3)
                                     .broadcast_to([P, 2, 2, P]), ALU.is_equal)
                V_.tensor_scalar(slot_hot[:, b, :], sio[:, :], sidx[:, k, at(t)], tok[:, at(t)], ALU.is_equal,
                                 ALU.mult).then_inc(s_hot, 1)

            pair_iterations(dve, pair)
            dve.wait_ge(s_pl, 2 * T)
            V_.tensor_scalar(gidx[:, :], accp[:, 0:SLOTS], -1.0, 0.0, ALU.add, ALU.max).then_inc(s_rd, 1)
            link(V_.tensor_scalar(sv[:, :], accp[:, 0:SLOTS], 0.0, float(2 * N), ALU.is_equal, ALU.mult))
            V_.scalar_tensor_tensor(out=cidx[:, :], in0=accp[:, 0:SLOTS], scalar=-1.0, in1=sv[:, :], op0=ALU.add,
                                    op1=ALU.add).then_inc(s_rd, 1)

            SLOT_LINKS = 2

            def split_lo(s, r, b, n):
                wait_apart(dve, (s_whi, s * 2 + (n + 1)))
                V_.tensor_tensor(wup[:, r % 2, n, 1, :], wexp[:, one(b), n, :].rearrange("p o f -> p (o f)"),
                                 wup[:, r % 2, n, 0, :].bitcast(F32), ALU.subtract).then_inc(s_wlo, 1)

            def tokens_lo(s, r, st):
                dve.wait_ge(s_fxe, s + 1)
                V_.tensor_tensor(xT[:, r, 1, :], tp[:, 0:F], xT[:, r, 0, :].bitcast(F32), ALU.subtract).then_inc(s_fxl, 1)

            dve.wait_ge(s_tab, 3)
            for k in range(2):
                b = table(dve, BUF, k)
                for n in range(2):
                    split_lo(k, k, b, n)
                if k == 0:
                    tokens_lo(0, 0, 0)
            slot_base = done[0]

            def slot(s, r, m, st):
                done[0] = slot_base + s * SLOT_LINKS
                two_on = st is None or st + 2 < SLOTS
                if two_on:
                    b = table(dve, BUF, s + 2)
                if st is None or st < SLOTS:
                    dve.wait_ge(s_fs, s + 1)
                    dve.wait_ge(s_fh, s * 2 + 2)
                    if st is None or st >= 1:
                        dve.wait_ge(s_fth, s)
                    V_.tensor_tensor(hid[:, :], nb[:, :], sil[:, :], ALU.mult).then_inc(s_fm, 1)
                if st is None or st + 1 < SLOTS:
                    tokens_lo(s + 1, (r + 1) % WR, st)
                if two_on:
                    for n in range(2):
                        split_lo(s + 2, (r + 2) % WR, b, n)
                if st is None or st >= 1:
                    v = (r - 1) % WR
                    dve.wait_ge(s_fy, s)
                    dve.wait_ge(s_lw, s)
                    if st is None or st >= WR + 1:
                        dve.wait_ge(s_sc, (s - WR) * 16)
                    V_.tensor_scalar(ysc[:, v, :], accp[:, 0:F], lanew[:, v, 0:1], None, ALU.mult).then_inc(s_fo, 1)
                if st is None or st < SLOTS:
                    dve.wait_ge(s_g[r], m * 16 + 16)
                    if st is None or st >= WR:
                        dve.wait_ge(s_fo, s - (WR - 1))
                    e = esl[:, at(s)]
                    link(V_.tensor_scalar(lanew[:, r, 0:1], xg[:, r, F + 2:F + 3], e, xg[:, r, F:F + 1],
                                          ALU.is_equal, ALU.mult))
                    link(V_.tensor_scalar(lanew[:, r, 1:2], xg[:, r, F + 3:F + 4], e, xg[:, r, F + 1:F + 2],
                                          ALU.is_equal, ALU.mult))
                    V_.tensor_tensor(lanew[:, r, 0:1], lanew[:, r, 0:1], lanew[:, r, 1:2], ALU.add).then_inc(s_lw, 1)

            slot_iterations(dve, slot)

        @block.tensor
        def _(pe):
            mm = nc.tensor.matmul
            tr = lambda o, i: nc.tensor.transpose(o, i, ident[:, :])

            def transpose_gru_weights(m):
                pe.wait_ge(s_wn, 16 * (m + 1))
                for n in range(2 * KB):
                    kb, half = n // 2, n % 2
                    if m or n >= 2:
                        pe.wait_ge(s_wev, 2 * KB * m + n - 1)
                    for r in range(3):
                        ins = tr((accp, accm)[n % 2][:, r * P:(r + 1) * P],
                                 wnat[:, half * 3 + r, kb * P:(kb + 1) * P])
                    ins.then_inc(s_wtr, 1)

            pe.wait_ge(s_const, CONSTS)
            transpose_gru_weights(0)
            transpose_gru_weights(1)
            pe.wait_ge(s_wx, 3 * KB)
            pe.wait_ge(s_wev, 4 * KB)

            def values(i, r, g, st, par):
                if live(st, 1):
                    pe.wait_ge(s_xe, i)
                    if after(st, 1, 4):
                        pe.wait_ge(s_lo, (i - 4) * 2)
                    for kb in range(KB):
                        ins = mm(wh_bank(r - 1)[:, 0:WXW], hT[:, KB * ((r - 1) % 2) + kb, :], Wx[:, kb, :],
                                 start=kb == 0, stop=kb == KB - 1)
                    ins.then_inc(s_wh, 1)
                if live(st, 0):
                    pe.wait_ge(s_xn, i + 1)
                    if after(st, 0, 2):
                        pe.wait_ge(s_xe, i - 1)
                    p = r % 2
                    for kb in range(KB):
                        ins = tr((tp, tp2)[p][:, kb * P:(kb + 1) * P], xnb[:, p, kb * P:(kb + 1) * P])
                    ins.then_inc(s_xt, 1)
                if r == 2 and (st is None or st > 2):
                    pe.wait_ge(s_dc, g)
                    mm(dbc, onesf[:, :], scr[:, 0:4 * P], start=True, stop=True).then_inc(s_db, 1)

            tile_iterations(pe, values)
            pe.wait_ge(s_dpe, T // 4)

            def transpose_adj(i, c, st):
                C = i * CPT + c
                q = c // CQ
                pe.wait_ge(s_t, i * Q + (q + 1))
                if st is None or st * CPT + c >= 2:
                    pe.wait_ge(s_mask, C - 1)
                for b in range(JB):
                    at0 = (c % CQ) * MC + b * P
                    ins = nc.tensor.transpose(pT[c % 2][:, b * P:(b + 1) * P], tbuf[:, q % 2, at0:at0 + P],
                                              identb[:, :])
                ins.then_inc(s_tr, 1)

            def accumulate(i, c, st):
                pe.wait_ge(s_mask, i * CPT + (c + 1))
                if c == 0 and after(st, 0, 1):
                    pe.wait_ge(s_af, i)
                for b in range(JB):
                    j = c * JB + b
                    for k, acc in enumerate((accp, accm)):
                        for part in range(2):
                            ins = mm(acc[:, 0:VW], mask[:, c % 2, k, b * P:(b + 1) * P], V[:, j, 2 * k + part, :],
                                     start=j == 0 and part == 0, stop=j == T - 1 and part == 1)
                ins.then_inc(s_mm, 1)

            def transpose_h(i, u, st):
                v = (u + 1) % 2
                pe.wait_ge(s_hp, i)
                pe.wait_ge(s_xb, i)
                if after(st, 1, 1):
                    pe.wait_ge(s_hT, i - 1)
                for n, src in enumerate((hp, xnb[:, v, :])):
                    for kb in range(KB):
                        ins = tr(tp[:, (n * KB + kb) * P:(n * KB + kb + 1) * P], src[:, kb * P:(kb + 1) * P])
                ins.then_inc(s_th, 1)

            def gru(i, st):
                pe.wait_ge(s_hT, i - 1)
                if after(st, 2, 1):
                    pe.wait_ge(s_gf, i - 2)
                for n in range(2 * KB):
                    mm(rzb[:, :], hT[:, n, :], wT[:, n // KB, n % KB, 0:2 * F], start=n == 0, stop=n == 2 * KB - 1)
                for n in range(2 * KB):
                    m, kb = n // KB, n % KB
                    ins = mm(nb[:, m * F:(m + 1) * F], hT[:, n, :], wT[:, m, kb, 2 * F:3 * F], start=kb == 0,
                             stop=kb == KB - 1)
                ins.then_inc(s_gru, 1)

            def transpose_x2(i, u, st):
                v = (u + 1) % 2
                pe.wait_ge(s_ln2, i - 2)
                if after(st, 3, 1):
                    pe.wait_ge(s_lg, i - 3)
                for kb in range(KB):
                    ins = tr(tp2[:, kb * P:(kb + 1) * P], xrow[:, v, kb * P:(kb + 1) * P])
                ins.then_inc(s_t2, 1)

            def gate(i):
                pe.wait_ge(s_t2e, i - 2)
                for kb in range(KB):
                    ins = mm(tp2[:, F:F + NE], xn2T[:, kb, :], gwt[:, kb, :], start=kb == 0, stop=kb == KB - 1)
                ins.then_inc(s_lgt, 1)

            pe.wait_ge(s_vd, 2)
            pe.wait_ge(s_lo, 2 * T)
            transpose_adj(0, 0, 0)

            def body(i, u, h, st):
                if live(st, 2):
                    gru(i, st)
                if live(st, 3):
                    transpose_x2(i, u, st)
                if live(st, 3) and not live(st, 0):
                    gate(i)
                for c in range(CPT):
                    if live(st, 0):
                        if c + 1 < CPT:
                            transpose_adj(i, c + 1, st)
                        elif st is None or st + 1 < T:
                            transpose_adj(i + 1, 0, None if st is None else st + 1)
                        accumulate(i, c, st)
                    if c == 0 and live(st, 3) and live(st, 0):
                        gate(i)
                    if c == min(2, CPT - 1) and live(st, 1):
                        transpose_h(i, u, st)

            graph_iterations(pe, body)

            pe.wait_ge(s_row, T)
            for lhs, acc in ((before, rzb), (onesb, nb)):
                for k in range(2):
                    ins = mm(acc[:, 0:T * NE], lhs[:, :], pick[:, k, :, :].rearrange("p t e -> p (t e)"), start=k == 0,
                             stop=k == 1)
                ins.then_inc(s_rk, 1)

            def place(t, k, b, st):
                pe.wait_ge(s_hot, t * 2 + (k + 1))
                mm(accp[:, 0:SLOTS + SLOTS % 2], lane_hot[:, b, :], slot_hot[:, b, :], start=st == 0 and k == 0,
                   stop=st == T - 1 and k == 1).then_inc(s_pl, 1)

            pair_iterations(pe, place)

            def transpose_tokens(s, r, m, st):
                pe.wait_ge(s_g[r], m * 16 + 16)
                if st is None or st >= 1:
                    pe.wait_ge(s_fxl, s)
                for k in range(KB):
                    ins = tr(tp[:, k * P:(k + 1) * P], xg[:, r, k:F:KB])
                ins.then_inc(s_ftx, 1)

            pe.wait_ge(s_tab, 3)
            transpose_tokens(0, 0, 0, 0)

            def slot(s, r, m, st):
                here = st is None or st < SLOTS
                if here:
                    pe.wait_ge(s_fxl, s + 1)
                    for n, acc in enumerate((rzb, nb)):
                        if st is None or st >= 1:
                            pe.wait_ge((s_fs, s_fm)[n], s)
                        pe.wait_ge(s_wlo, s * 2 + (n + 1))
                        terms = [(k, a, b) for k in range(KB) for a, b in ((0, 0), (1, 0), (0, 1))]
                        for k, a, b in terms:
                            ins = mm(acc[:, 0:HID], xT[:, r, a, k * P:(k + 1) * P],
                                     wup[:, r % 2, n, b, k * HID:(k + 1) * HID], start=(k, a, b) == terms[0],
                                     stop=(k, a, b) == terms[-1])
                        ins.then_inc(s_fh, 1)
                if st is None or st + 1 < SLOTS:
                    transpose_tokens(s + 1, (r + 1) % WR, m + (r + 1) // WR, None if st is None else st + 1)
                if st is None or st >= 1:
                    b1 = table(pe, BUF, s - 1)
                    pe.wait_ge(s_fte, s)
                    if st is None or st >= 2:
                        pe.wait_ge(s_fo, s - 1)
                    else:
                        pe.wait_ge(s_rd, 2)
                    for k in range(HB):
                        ins = mm(accp[:, 0:F], hidT[:, k, :],
                                 wexp[:, one(b1), 2, k * F:(k + 1) * F].rearrange("p o f -> p (o f)"), start=k == 0,
                                 stop=k == HB - 1)
                    ins.then_inc(s_fy, 1)
                if here:
                    pe.wait_ge(s_fm, s + 1)
                    if st is None or st >= 1:
                        pe.wait_ge(s_fte, s)
                    for k in range(HB):
                        ins = tr(tp2[:, k * P:(k + 1) * P], hid[:, k:HID:HB])
                    ins.then_inc(s_fth, 1)

            slot_iterations(pe, slot)


INS = ["x", "adj", "L0_gnn_W", "L0_gnn_a", "L0_gnn_w_ih", "L0_gnn_w_hh", "L0_gnn_b_ih", "L0_gnn_b_hh",
       "L0_ffn_gate_w", "L0_ffn_gate_b", "L0_ffn_w1", "L0_ffn_w2", "L0_ffn_w3"]


def kernel(**inputs):
    import numpy as np
    import concourse.bacc as bacc
    from concourse.bass_utils import run_bass_kernel_spmd

    nc = bacc.Bacc("TRN2", target_bir_lowering=False, num_devices=1)
    arrays, args = {}, []
    for name in INS:
        v = np.ascontiguousarray(inputs[name])
        arrays["in_" + name] = v
        args.append(nc.dram_tensor("in_" + name, v.shape, mybir.dt.from_np(v.dtype), kind="ExternalInput").ap())
    n, f = inputs["x"].shape
    out = nc.dram_tensor("out", (n, f), F32, kind="ExternalOutput").ap()
    rows = nc.dram_tensor("token_rows", (n, f + 4), F32, kind="Internal").ap()
    gnn_moe(nc, *args, out, rows)
    return run_bass_kernel_spmd(nc, [arrays], core_ids=[0]).results[0]["out"]
```
